# Optimizing a Trainium2 kernel written in Bass

```python
import numpy as np
import jax
import jax.numpy as jnp

def _softmax(x, axis=-1):
    return jax.nn.softmax(x, axis=axis)

def _gelu(x):
    return jax.nn.gelu(x, approximate=True)

def _silu(x):
    return jax.nn.silu(x)

def _sigmoid(x):
    return jax.nn.sigmoid(x)

def _layernorm(x, axis=-1, eps=1e-05):
    m = jnp.mean(x, axis=axis, keepdims=True)
    v = jnp.var(x, axis=axis, keepdims=True)
    return (x - m) / jnp.sqrt(v + eps)

def _scatter_add(tgt, idx, src, axis=0):
    return tgt.at[idx].add(src)

def _segment_sum(src, seg, n):
    return jax.ops.segment_sum(src, seg, n)
kernel_name = 'mk_xattn_seq_d2_seqx_r8_c2427f'

def setup_inputs(seed: int=0):
    np.random.seed(seed)
    _w = jnp.asarray

    def _rec_inputs():
        import jax
        import jax.numpy as jnp
        _rk = jax.random.key(seed)
        x = -0.0001108 + 0.9999 * jax.random.normal(jax.random.fold_in(_rk, 1), (8, 256, 160), jnp.float32)
        _lenS = 256 - jax.random.randint(jax.random.fold_in(_rk, 7), (8,), 0, max(1, 256 // 4) + 1, jnp.int32)
        _lenS2 = 512 - jax.random.randint(jax.random.fold_in(_rk, 8), (8,), 0, max(1, 512 // 4) + 1, jnp.int32)
        _ctx_2048P = jax.random.normal(jax.random.fold_in(_rk, 11), (8, 16, 256), jnp.float32)
        _ctx_2048c = jax.random.dirichlet(jax.random.fold_in(_rk, 511), 0.3 * jnp.ones((16,), jnp.float32), (8, 512))
        _ctx_2048t = jnp.einsum('bsk,bkd->bsd', _ctx_2048c, _ctx_2048P)
        _ctx_2048t = _ctx_2048t * jax.lax.rsqrt(jnp.mean(jnp.square(_ctx_2048t)) + 1e-12) * 0.953939
        ctx_2048 = -0.000395056 + 1.00006 * (_ctx_2048t + 0.3 * jax.random.normal(jax.random.fold_in(_rk, 611), (8, 512, 256), jnp.float32))
        return (x, ctx_2048)
    x, ctx_2048 = _rec_inputs()

    def _L0_xattn_setup():
        import jax, jax.numpy as jnp
        import numpy as np
        NUM_HEADS = 20
        TEXT_LEN = 77
        IP_SCALE = 1.0

        def _attend(q, k, v, sm_scale):
            scores = jnp.einsum('bhsd,bhld->bhsl', q, k) * sm_scale
            probs = jax.nn.softmax(scores, axis=-1)
            return jnp.einsum('bhsl,bhld->bhsd', probs, v)

        def _split_heads(x, h):
            b, s, c = x.shape
            return x.reshape(b, s, h, c // h).transpose(0, 2, 1, 3)

        def _merge_heads(x):
            b, h, s, d = x.shape
            return x.transpose(0, 2, 1, 3).reshape(b, s, h * d)
        key = jax.random.key(seed)
        ks = jax.random.split(key, 8)
        B, S, C, CC, L = (8, 512, 160, 256, TEXT_LEN + 4)
        sd_q = 1.0 / np.sqrt(C)
        sd_kv = 1.0 / np.sqrt(CC)
        return {'hidden_states': jax.random.normal(ks[0], (B, S, C), jnp.float32), 'encoder_hidden_states': jax.random.normal(ks[1], (B, L, CC), jnp.float32), 'Wq': jax.random.normal(ks[2], (C, C), jnp.float32) * sd_q, 'Wk': jax.random.normal(ks[3], (C, CC), jnp.float32) * sd_kv, 'Wv': jax.random.normal(ks[4], (C, CC), jnp.float32) * sd_kv, 'Wk_ip': jax.random.normal(ks[5], (C, CC), jnp.float32) * sd_kv, 'Wv_ip': jax.random.normal(ks[6], (C, CC), jnp.float32) * sd_kv, 'Wo': jax.random.normal(ks[7], (C, C), jnp.float32) * sd_q, 'bo': jnp.zeros((C,), jnp.float32)}
    _L0_xattn_all = _L0_xattn_setup()
    _L0_xattn_in = {k: v for k, v in _L0_xattn_all.items() if k in ('Wq', 'Wk', 'Wv', 'Wk_ip', 'Wv_ip', 'Wo', 'bo')}
    del _L0_xattn_all

    def _L1_xattn_setup():
        import jax, jax.numpy as jnp
        import numpy as np
        DIM = 160
        HEADS = 20
        DHEAD = 64
        CTX_DIM = 256
        INNER = HEADS * DHEAD
        FF_INNER = 4 * DIM
        SCALE = DHEAD ** (-0.5)
        EPS = 1e-05

        def _layer_norm(x, g, b):
            m = jnp.mean(x, axis=-1, keepdims=True)
            v = jnp.mean(jnp.square(x - m), axis=-1, keepdims=True)
            return (x - m) * jax.lax.rsqrt(v + EPS) * g + b

        def _attention(x, ctx, wq, wk, wv, wo, bo):
            B, N, _ = x.shape
            M = ctx.shape[1]
            q = (x @ wq).reshape(B, N, HEADS, DHEAD).transpose(0, 2, 1, 3)
            k = (ctx @ wk).reshape(B, M, HEADS, DHEAD).transpose(0, 2, 1, 3)
            v = (ctx @ wv).reshape(B, M, HEADS, DHEAD).transpose(0, 2, 1, 3)
            sim = jnp.einsum('bhid,bhjd->bhij', q, k) * SCALE
            attn = jax.nn.softmax(sim, axis=-1)
            out = jnp.einsum('bhij,bhjd->bhid', attn, v)
            out = out.transpose(0, 2, 1, 3).reshape(B, N, INNER)
            return out @ wo + bo

        def _geglu_ff(x, w1, b1, w2, b2):
            h = x @ w1 + b1
            a, gate = jnp.split(h, 2, axis=-1)
            return a * jax.nn.gelu(gate, approximate=False) @ w2 + b2
        key = jax.random.key(seed)
        ks = jax.random.split(key, 16)
        s = 0.02
        d = {'x': jax.random.normal(ks[0], (2, 256, DIM), jnp.float32), 'context': jax.random.normal(ks[1], (2, 77, CTX_DIM), jnp.float32), 'a1_wq': jax.random.normal(ks[2], (DIM, INNER), jnp.float32) * s, 'a1_wk': jax.random.normal(ks[3], (DIM, INNER), jnp.float32) * s, 'a1_wv': jax.random.normal(ks[4], (DIM, INNER), jnp.float32) * s, 'a1_wo': jax.random.normal(ks[5], (INNER, DIM), jnp.float32) * s, 'a1_bo': jnp.zeros((DIM,), jnp.float32), 'a2_wq': jax.random.normal(ks[6], (DIM, INNER), jnp.float32) * s, 'a2_wk': jax.random.normal(ks[7], (CTX_DIM, INNER), jnp.float32) * s, 'a2_wv': jax.random.normal(ks[8], (CTX_DIM, INNER), jnp.float32) * s, 'a2_wo': jax.random.normal(ks[9], (INNER, DIM), jnp.float32) * s, 'a2_bo': jnp.zeros((DIM,), jnp.float32), 'ff_w1': jax.random.normal(ks[10], (DIM, 2 * FF_INNER), jnp.float32) * s, 'ff_b1': jnp.zeros((2 * FF_INNER,), jnp.float32), 'ff_w2': jax.random.normal(ks[11], (FF_INNER, DIM), jnp.float32) * s, 'ff_b2': jnp.zeros((DIM,), jnp.float32), 'ln1_g': jnp.ones((DIM,), jnp.float32), 'ln1_b': jnp.zeros((DIM,), jnp.float32), 'ln2_g': jnp.ones((DIM,), jnp.float32), 'ln2_b': jnp.zeros((DIM,), jnp.float32), 'ln3_g': jnp.ones((DIM,), jnp.float32), 'ln3_b': jnp.zeros((DIM,), jnp.float32)}
        return d
    _L1_xattn_all = _L1_xattn_setup()
    _L1_xattn_in = {k: v for k, v in _L1_xattn_all.items() if k in ('a1_wq', 'a1_wk', 'a1_wv', 'a1_wo', 'a1_bo', 'a2_wq', 'a2_wk', 'a2_wv', 'a2_wo', 'a2_bo', 'ff_w1', 'ff_b1', 'ff_w2', 'ff_b2', 'ln1_g', 'ln1_b', 'ln2_g', 'ln2_b', 'ln3_g', 'ln3_b')}
    del _L1_xattn_all
    return {'x': x, 'ctx_2048': ctx_2048, 'L0_xattn_Wq': _L0_xattn_in['Wq'], 'L0_xattn_Wk': _L0_xattn_in['Wk'], 'L0_xattn_Wv': _L0_xattn_in['Wv'], 'L0_xattn_Wk_ip': _L0_xattn_in['Wk_ip'], 'L0_xattn_Wv_ip': _L0_xattn_in['Wv_ip'], 'L0_xattn_Wo': _L0_xattn_in['Wo'], 'L0_xattn_bo': _L0_xattn_in['bo'], 'L1_xattn_a1_wq': _L1_xattn_in['a1_wq'], 'L1_xattn_a1_wk': _L1_xattn_in['a1_wk'], 'L1_xattn_a1_wv': _L1_xattn_in['a1_wv'], 'L1_xattn_a1_wo': _L1_xattn_in['a1_wo'], 'L1_xattn_a1_bo': _L1_xattn_in['a1_bo'], 'L1_xattn_a2_wq': _L1_xattn_in['a2_wq'], 'L1_xattn_a2_wk': _L1_xattn_in['a2_wk'], 'L1_xattn_a2_wv': _L1_xattn_in['a2_wv'], 'L1_xattn_a2_wo': _L1_xattn_in['a2_wo'], 'L1_xattn_a2_bo': _L1_xattn_in['a2_bo'], 'L1_xattn_ff_w1': _L1_xattn_in['ff_w1'], 'L1_xattn_ff_b1': _L1_xattn_in['ff_b1'], 'L1_xattn_ff_w2': _L1_xattn_in['ff_w2'], 'L1_xattn_ff_b2': _L1_xattn_in['ff_b2'], 'L1_xattn_ln1_g': _L1_xattn_in['ln1_g'], 'L1_xattn_ln1_b': _L1_xattn_in['ln1_b'], 'L1_xattn_ln2_g': _L1_xattn_in['ln2_g'], 'L1_xattn_ln2_b': _L1_xattn_in['ln2_b'], 'L1_xattn_ln3_g': _L1_xattn_in['ln3_g'], 'L1_xattn_ln3_b': _L1_xattn_in['ln3_b']}

def reference(x, ctx_2048, L0_xattn_Wq, L0_xattn_Wk, L0_xattn_Wv, L0_xattn_Wk_ip, L0_xattn_Wv_ip, L0_xattn_Wo, L0_xattn_bo, L1_xattn_a1_wq, L1_xattn_a1_wk, L1_xattn_a1_wv, L1_xattn_a1_wo, L1_xattn_a1_bo, L1_xattn_a2_wq, L1_xattn_a2_wk, L1_xattn_a2_wv, L1_xattn_a2_wo, L1_xattn_a2_bo, L1_xattn_ff_w1, L1_xattn_ff_b1, L1_xattn_ff_w2, L1_xattn_ff_b2, L1_xattn_ln1_g, L1_xattn_ln1_b, L1_xattn_ln2_g, L1_xattn_ln2_b, L1_xattn_ln3_g, L1_xattn_ln3_b):
    import jax
    import jax.numpy as jnp

    def _L0_xattn_ref(hidden_states, encoder_hidden_states, Wq, Wk, Wv, Wk_ip, Wv_ip, Wo, bo):
        import jax, jax.numpy as jnp
        import numpy as np
        NUM_HEADS = 20
        TEXT_LEN = 77
        IP_SCALE = 1.0

        def _attend(q, k, v, sm_scale):
            scores = jnp.einsum('bhsd,bhld->bhsl', q, k) * sm_scale
            probs = jax.nn.softmax(scores, axis=-1)
            return jnp.einsum('bhsl,bhld->bhsd', probs, v)

        def _split_heads(x, h):
            b, s, c = x.shape
            return x.reshape(b, s, h, c // h).transpose(0, 2, 1, 3)

        def _merge_heads(x):
            b, h, s, d = x.shape
            return x.transpose(0, 2, 1, 3).reshape(b, s, h * d)
        residual = hidden_states
        B, S, C = hidden_states.shape
        H = NUM_HEADS
        D = C // H
        sm_scale = 1.0 / jnp.sqrt(jnp.asarray(D, hidden_states.dtype))
        text = encoder_hidden_states[:, :TEXT_LEN, :]
        ip = encoder_hidden_states[:, TEXT_LEN:, :]
        q = _split_heads(hidden_states @ Wq.T, H)
        k = _split_heads(text @ Wk.T, H)
        v = _split_heads(text @ Wv.T, H)
        out_text = _merge_heads(_attend(q, k, v, sm_scale))
        k_ip = _split_heads(ip @ Wk_ip.T, H)
        v_ip = _split_heads(ip @ Wv_ip.T, H)
        out_ip = _merge_heads(_attend(q, k_ip, v_ip, sm_scale))
        out = out_text + IP_SCALE * out_ip
        out = out @ Wo.T + bo
        return out + residual

    def _L1_xattn_ref(x, context, a1_wq, a1_wk, a1_wv, a1_wo, a1_bo, a2_wq, a2_wk, a2_wv, a2_wo, a2_bo, ff_w1, ff_b1, ff_w2, ff_b2, ln1_g, ln1_b, ln2_g, ln2_b, ln3_g, ln3_b):
        import jax, jax.numpy as jnp
        import numpy as np
        DIM = 160
        HEADS = 20
        DHEAD = 64
        CTX_DIM = 256
        INNER = HEADS * DHEAD
        FF_INNER = 4 * DIM
        SCALE = DHEAD ** (-0.5)
        EPS = 1e-05

        def _layer_norm(x, g, b):
            m = jnp.mean(x, axis=-1, keepdims=True)
            v = jnp.mean(jnp.square(x - m), axis=-1, keepdims=True)
            return (x - m) * jax.lax.rsqrt(v + EPS) * g + b

        def _attention(x, ctx, wq, wk, wv, wo, bo):
            B, N, _ = x.shape
            M = ctx.shape[1]
            q = (x @ wq).reshape(B, N, HEADS, DHEAD).transpose(0, 2, 1, 3)
            k = (ctx @ wk).reshape(B, M, HEADS, DHEAD).transpose(0, 2, 1, 3)
            v = (ctx @ wv).reshape(B, M, HEADS, DHEAD).transpose(0, 2, 1, 3)
            sim = jnp.einsum('bhid,bhjd->bhij', q, k) * SCALE
            attn = jax.nn.softmax(sim, axis=-1)
            out = jnp.einsum('bhij,bhjd->bhid', attn, v)
            out = out.transpose(0, 2, 1, 3).reshape(B, N, INNER)
            return out @ wo + bo

        def _geglu_ff(x, w1, b1, w2, b2):
            h = x @ w1 + b1
            a, gate = jnp.split(h, 2, axis=-1)
            return a * jax.nn.gelu(gate, approximate=False) @ w2 + b2
        n = _layer_norm(x, ln1_g, ln1_b)
        x = x + _attention(n, n, a1_wq, a1_wk, a1_wv, a1_wo, a1_bo)
        n = _layer_norm(x, ln2_g, ln2_b)
        x = x + _attention(n, context, a2_wq, a2_wk, a2_wv, a2_wo, a2_bo)
        x = _geglu_ff(_layer_norm(x, ln3_g, ln3_b), ff_w1, ff_b1, ff_w2, ff_b2) + x
        return x
    x = _L0_xattn_ref(x, ctx_2048, L0_xattn_Wq, L0_xattn_Wk, L0_xattn_Wv, L0_xattn_Wk_ip, L0_xattn_Wv_ip, L0_xattn_Wo, L0_xattn_bo)
    x = _L1_xattn_ref(x, ctx_2048, L1_xattn_a1_wq, L1_xattn_a1_wk, L1_xattn_a1_wv, L1_xattn_a1_wo, L1_xattn_a1_bo, L1_xattn_a2_wq, L1_xattn_a2_wk, L1_xattn_a2_wv, L1_xattn_a2_wo, L1_xattn_a2_bo, L1_xattn_ff_w1, L1_xattn_ff_b1, L1_xattn_ff_w2, L1_xattn_ff_b2, L1_xattn_ln1_g, L1_xattn_ln1_b, L1_xattn_ln2_g, L1_xattn_ln2_b, L1_xattn_ln3_g, L1_xattn_ln3_b)
    return x

_drawn_inputs = setup_inputs


def setup_inputs(seed=0):
    import zlib

    import numpy as np

    out = dict(_drawn_inputs(seed))
    spreads = {'L0_xattn_bo': (0.0, 0.1),
     'L1_xattn_a1_bo': (0.0, 0.1),
     'L1_xattn_a2_bo': (0.0, 0.1),
     'L1_xattn_ff_b1': (0.0, 0.8),
     'L1_xattn_ff_b2': (0.0, 0.1),
     'L1_xattn_ln1_g': (1.0, 0.6),
     'L1_xattn_ln1_b': (0.0, 0.522),
     'L1_xattn_ln2_g': (1.0, 0.6),
     'L1_xattn_ln2_b': (0.0, 0.8),
     'L1_xattn_ln3_g': (1.0, 0.6),
     'L1_xattn_ln3_b': (0.0, 0.8)}
    factors = {'L1_xattn_a1_wq': 8.0,
     'L1_xattn_a1_wk': 8.0,
     'L1_xattn_a2_wq': 8.0,
     'L1_xattn_a2_wk': 8.0,
     'L1_xattn_ff_w1': 3.596,
     'L1_xattn_ff_w2': 3.529}
    for name, (base, spread) in spreads.items():
        noise = np.random.default_rng([zlib.crc32(name.encode()), seed]).standard_normal(out[name].shape)
        drawn = base * np.exp(spread * noise) if base else spread * noise
        out[name] = jnp.asarray(drawn.astype(out[name].dtype))
    for name, factor in factors.items():
        out[name] = (out[name] * factor).astype(out[name].dtype)
    return out
```

```python
import numpy as np
import concourse.bass as bass
from concourse import mybir
from contextlib import ExitStack

FP32 = mybir.dt.float32
FP32R = mybir.dt.float32r
BF16 = mybir.dt.bfloat16
ALU = mybir.AluOpType
ACT = mybir.ActivationFunctionType
AX = mybir.AxisListType

B, SQ, C = 8, 256, 160
SK, CC = 512, 256
TEXT = 77
HEADS = 20
D0 = C // HEADS
D1 = 64
INNER = HEADS * D1
FF = 4 * C
P = 128
QT = SQ // P
REST = C - P
EXT = 3 * REST
PAIRS = HEADS // 2
EPS = 1e-5

N_TERMS = [(0, 0, P), (1, 0, P), (0, 1, P), (2, 2, EXT)]
CTX_TERMS = [(0, 0, P), (1, 1, P), (2, 0, P), (3, 1, P), (0, 2, P), (1, 3, P)]


def wait(eng, sem, value):
    if isinstance(value, int) and value <= 0:
        return
    eng.wait_ge(sem, value)


def over_batches(eng, body):
    body(0)
    with eng.Fori(1, B - 1) as b:
        body(b)
    body(B - 1)


def is_last(b):
    return isinstance(b, int) and b == B - 1


def split_weights(nc, sems, staging, pieces):
    loaded, rounded, done = sems

    def load(sp):
        for k, (src, rows, _, _, _) in enumerate(pieces):
            wait(sp, done, k - 1)
            sp.dma_start(staging[0:rows, k % 2, 0:src.shape[1]], src).then_inc(loaded[k % 2], 16)

    def high(act):
        for k, (src, rows, hi, _, _) in enumerate(pieces):
            act.wait_ge(loaded[k % 2], 16 * (k // 2 + 1))
            nc.scalar.activation(hi, staging[0:rows, k % 2, 0:src.shape[1]], ACT.Copy).then_inc(rounded, 1)

    def low(dve):
        for k, (src, rows, hi, lo, lo_rows) in enumerate(pieces):
            r0, r1 = lo_rows
            dve.wait_ge(rounded, k + 1)
            minus = lo if lo_rows != (0, rows) else hi
            nc.vector.tensor_tensor(lo, staging[r0:r1, k % 2, 0:src.shape[1]], minus.bitcast(FP32),
                                    ALU.subtract).then_inc(done, 1)

    return load, high, low


def n_weight_pieces(src_main, src_ext, slots):
    return [(src_main, P, slots[:, 0, :], slots[:, 1, :], (0, P)),
            (src_ext, EXT, slots[0:EXT, 2, :], slots[REST:2 * REST, 2, :], (REST, 2 * REST))]


class LayerNorm:

    def __init__(self, nc, ctx, tag, xs, ident, n_terms, gains, bias_rows, psum):
        sb = lambda name, shape, dt: ctx.enter_context(nc.sbuf_tensor(f"{tag}_{name}", shape, dt))
        sem = lambda name: ctx.enter_context(nc.semaphore(f"{tag}_{name}"))
        self.nc, self.xs, self.ident, self.nt, self.gains, self.rows, self.psum = (
            nc, xs, ident, n_terms, gains, bias_rows, psum)
        self.stats = sb("stats", [P, QT, 6], FP32)
        self.mv = sb("mv", [P, QT, 2], FP32)
        self.var = sb("var", [P, QT], FP32)
        self.aggregated = sb("aggregated", [P, 1], FP32)
        self.rstd = sb("rstd", [P, QT], FP32)
        self.half = sb("half", [P, QT], FP32)
        self.xhat = sb("xhat", [P, QT, P + EXT], FP32)
        self.n32 = sb("n32", [P, 2, SQ], FP32)
        self.half_set = sem("half_set")
        self.stats_chain = sem("stats_chain")
        self.var_ready = sem("var_ready")
        self.rstd_ready = sem("rstd_ready")
        self.xhat_ready = sem("xhat_ready")
        self.biased = sem("biased")
        self.t_ready = sem("t_ready")
        self.n32_ready = sem("n32_ready")
        self.n_hi = sem("n_hi")
        self.n_ready = sem("n_ready")

    def pool_setup(self, pool):
        self.nc.gpsimd.memset(self.half[:], -0.5).then_inc(self.half_set, 1)
        pool.wait_ge(self.half_set, 1)

    def dve_stats(self, dve, m):
        nc = self.nc
        for qt in range(QT):
            last = nc.vector.bn_stats(self.stats[:, qt], self.xs[:, m, qt])
        last.then_inc(self.stats_chain, 1)
        wait(dve, self.stats_chain, 2 * m + 1)
        nc.vector.memset(self.aggregated[:], 0.0)
        for qt in range(QT):
            last = nc.vector.bn_aggr(self.mv[:, qt], self.stats[:, qt])
        last.then_inc(self.stats_chain, 1)
        wait(dve, self.stats_chain, 2 * m + 2)
        nc.vector.tensor_scalar(self.var[:], self.mv[:, :, 1], EPS, None, ALU.add).then_inc(self.var_ready, 1)

    def pool_rstd(self, pool, m):
        pool.wait_ge(self.var_ready, m + 1)
        self.nc.gpsimd.tensor_tensor(self.rstd[:], self.var[:], self.half[:], ALU.pow).then_inc(self.rstd_ready, 1)

    def dve_xhat(self, dve, m):
        nc = self.nc
        dve.wait_ge(self.rstd_ready, m + 1)
        for qt in range(QT):
            scalars = (self.mv[:, qt, 0:1], self.rstd[:, qt:qt + 1])
            nc.vector.tensor_scalar(self.xhat[:, qt, 0:C], self.xs[:, m, qt], *scalars, ALU.subtract, ALU.mult)
            for r in range(1, 3):
                last = nc.vector.tensor_scalar(self.xhat[:, qt, P + r * REST:P + (r + 1) * REST],
                                               self.xs[:, m, qt, P:C], *scalars, ALU.subtract, ALU.mult)
        last.then_inc(self.xhat_ready, 1)
        dve.wait_ge(self.xhat_ready, m + 1)
        nc.vector.tensor_tensor(self.xs[:, m], self.xs[:, m], self.rows, ALU.add).then_inc(self.biased, 1)

    def pe_transpose(self, pe, m):
        nc = self.nc
        pe.wait_ge(self.xhat_ready, m + 1)
        for qt in range(QT):
            nc.tensor.transpose(self.psum[:, qt * P:(qt + 1) * P], self.xhat[:, qt, 0:P], self.ident)
        for qt in range(QT):
            last = nc.tensor.transpose(self.psum[0:EXT, SQ + qt * P:SQ + (qt + 1) * P],
                                       self.xhat[:, qt, P:P + EXT], self.ident)
        last.then_inc(self.t_ready, 1)

    def dve_n32(self, dve, m):
        nc = self.nc
        dve.wait_ge(self.t_ready, m + 1)
        g, gains = self.gains, nc.vector.tensor_scalar
        gains(self.n32[:, 0], self.psum[:, 0:SQ], g[:, 0:1], g[:, 1:2], ALU.mult, ALU.add)
        gains(self.n32[0:EXT, 1], self.psum[0:EXT, SQ:2 * SQ], g[0:EXT, 2:3], g[0:EXT, 3:4],
              ALU.mult, ALU.add).then_inc(self.n32_ready, 1)

    def act_hi(self, act, m):
        nc = self.nc
        act.wait_ge(self.n32_ready, m + 1)
        nc.scalar.activation(self.nt[:, 0], self.n32[:, 0], ACT.Copy)
        nc.scalar.activation(self.nt[0:EXT, 2], self.n32[0:EXT, 1], ACT.Copy).then_inc(self.n_hi, 1)

    def dve_lo(self, dve, m):
        nc = self.nc
        dve.wait_ge(self.n_hi, m + 1)
        nc.vector.tensor_tensor(self.nt[:, 1], self.n32[:, 0], self.nt[:, 0].bitcast(FP32), ALU.subtract)
        lo = self.nt[2 * REST:EXT, 2]
        nc.vector.tensor_tensor(lo, self.n32[2 * REST:EXT, 1], lo.bitcast(FP32),
                                ALU.subtract).then_inc(self.n_ready, 1)


def attention_layer(nc, tag, xs, ident, dram, ctx_t):
    cross = ctx_t is not None
    NK = SK if cross else SQ
    KT = NK // P
    KB = KT // 2
    NB = 2 * KB
    NS = 2 * QT if cross else 2
    KSLOTS = 4 if cross else 3
    K_TERMS = CTX_TERMS if cross else N_TERMS
    SCALE = float(D1) ** -0.5
    total = PAIRS * B

    with ExitStack() as ctx:
        sb = lambda name, shape, dt: ctx.enter_context(nc.sbuf_tensor(f"{tag}_{name}", shape, dt))
        ps = lambda name, shape: ctx.enter_context(nc.psum_tensor(f"{tag}_{name}", shape, FP32))
        sem = lambda name: ctx.enter_context(nc.semaphore(f"{tag}_{name}"))

        wq = sb("wq", [P, 3, INNER], FP32R)
        wk = sb("wk", [P, KSLOTS, INNER], FP32R)
        wv = sb("wv", [P, KSLOTS, INNER], FP32R)
        wo = sb("wo", [P, PAIRS, C], FP32)
        gains = sb("gains", [P, 4], FP32)
        bo_rows = sb("bo_rows", [P, QT, C], FP32)
        staging = sb("staging", [P, 2, INNER], FP32)
        ones = sb("ones", [P, D1], FP32)
        ones_b = sb("ones_b", [P, P], BF16)
        nt = sb("nt", [P, 3, SQ], FP32R)
        qh = sb("qh", [P, 2, SQ], FP32R)
        ql = sb("ql", [P, 2, SQ], FP32R)
        kh = sb("kh", [P, 2, 2, NK], FP32R)
        kl = sb("kl", [P, 2, 2, NK], FP32R)
        v = sb("v", [P, KT, INNER], FP32)
        negmax = sb("negmax", [P, 2, 2, QT], FP32)
        diag = sb("diag", [P, 2, 2, SQ], BF16)
        probs = sb("probs", [P, 2, 2, KT, SQ], FP32)
        half_sum = sb("half_sum", [P, 2, 2, 2, SQ], FP32)
        key_sum = sb("key_sum", [P, 2, 2, SQ], FP32)
        recip = sb("recip", [P, SQ], FP32)
        ot = sb("ot", [P, 2, SQ], FP32)
        if cross:
            ct32 = sb("ct32", [P, 2, NK], FP32)
            ct = sb("ct", [P, 4, NK], FP32R)
        pa, pb, pv, py = ps("pa", [P, 512]), ps("pb", [P, 512]), ps("pv", [P, 512]), ps("py", [P, 512])
        pscore = ps("pscore", [P, 2, 512])
        pst = ps("pst", [P, 2, 512])

        loaded = [sem("loaded0"), sem("loaded1")]
        rounded, w_done, small_in = sem("rounded"), sem("w_done"), sem("small_in")
        zeroed, ones_set = sem("zeroed"), sem("ones_set")
        ctx_in, c_hi, c_ready = sem("ctx_in"), sem("c_hi"), sem("c_ready")
        q_ready, q_hi, q_split = sem("q_ready"), sem("q_hi"), sem("q_split")
        k_ready, k_hi, k_split = sem("k_ready"), sem("k_hi"), sem("k_split")
        v_ready, v_copied = sem("v_ready"), sem("v_copied")
        score_ready, max_done, diag_ready = sem("score_ready"), sem("max_done"), sem("diag_ready")
        st_ready, exp_done = sem("st_ready"), sem("exp_done")
        half_done, sum_ready = sem("half_done"), sem("sum_ready")
        pv_done, recip_done, ot_ready = sem("pv_done"), sem("recip_done"), sem("ot_ready")
        y_acc, y_taken = sem("y_acc"), sem("y_taken")

        ln = LayerNorm(nc, ctx, f"{tag}_ln", xs, ident, nt, gains, bo_rows[:], pa)
        pieces = n_weight_pieces(dram["wq"], dram["wq_ext"], wq)
        if cross:
            for w, src in ((wk, dram["wk"]), (wv, dram["wv"])):
                for half in range(2):
                    pieces.append((src[half], P, w[:, half, :], w[:, 2 + half, :], (0, P)))
        else:
            pieces += n_weight_pieces(dram["wk"], dram["wk_ext"], wk)
            pieces += n_weight_pieces(dram["wv"], dram["wv_ext"], wv)
        load_w, high_w, low_w = split_weights(nc, (loaded, rounded, w_done), staging, pieces)

        def runs(b, t, lag):
            return not isinstance(b, int) or 0 <= PAIRS * b + t - lag < total

        def tail(body):
            for t in range(PAIRS, PAIRS + 4):
                body(B - 1, t)

        block = ctx.enter_context(nc.Block())

        @block.sync
        def _(sp):
            sp.dma_start(gains[:], dram["gains"]).then_inc(small_in, 16)
            sp.dma_start(bo_rows[:], dram["bo_rows"]).then_inc(small_in, 16)
            sp.dma_start(wo[:], dram["wo"]).then_inc(small_in, 16)
            if cross:
                sp.dma_start(ct32[:], ctx_t[0]).then_inc(ctx_in, 16)
            load_w(sp)
            if cross:
                with sp.Fori(1, B) as b:
                    sp.wait_ge(c_ready, b)
                    sp.dma_start(ct32[:], ctx_t[b]).then_inc(ctx_in, 16)

        @block.tensor
        def _(pe):
            mm = nc.tensor.matmul

            def scores(b, t, which):
                g1, par = PAIRS * b + t - 1, (t - 1) % 2
                for i in which:
                    n = NS * g1 + i
                    wait(pe, max_done, n - 1)
                    if cross:
                        last = mm(pscore[:, i % 2, :], qh[:, par, (i % QT) * P:(i % QT + 1) * P],
                                  kh[:, par, i // QT, :], start=True, stop=True)
                    else:
                        for qt in range(QT):
                            last = mm(pscore[:, i % 2, qt * NK:(qt + 1) * NK], qh[:, par, qt * P:(qt + 1) * P],
                                      kh[:, par, i, :], start=True, stop=True)
                    last.then_inc(score_ready, 1)

            def values(b, t, kb):
                bank = (pa, pb)[kb]
                acts = ct if cross else nt
                for j in range(2):
                    kt = 2 * kb + j
                    for i, (ws, xs_, rows) in enumerate(K_TERMS):
                        last = mm(bank[:, j * 256:(j + 1) * 256], acts[0:rows, xs_, kt * P:(kt + 1) * P],
                                  wv[0:rows, ws, t * P:t * P + 256], start=i == 0, stop=i == len(K_TERMS) - 1)
                last.then_inc(v_ready, 1)

            def step(b, t):
                g = PAIRS * b + t
                if runs(b, t, 2):
                    g2, par = g - 2, t % 2
                    wait(pe, diag_ready, 2 * (g2 + 1))
                    for h in range(2):
                        for kb in range(KB):
                            n = h * KB + kb
                            wait(pe, exp_done, NB * g2 + n - 1)
                            for j in range(2):
                                out = pst[:, n % 2, j * SQ:(j + 1) * SQ]
                                keys = slice((2 * kb + j) * P, (2 * kb + j + 1) * P)
                                mm(out, ones_b[:], diag[:, par, h, :], start=True, stop=False)
                                mm(out, kh[:, par, h, keys], qh[:, par, :], start=False, stop=False)
                                mm(out, kl[:, par, h, keys], qh[:, par, :], start=False, stop=False)
                                last = mm(out, kh[:, par, h, keys], ql[:, par, :], start=False, stop=True)
                            last.then_inc(st_ready, 1)
                if runs(b, t, 1):
                    wait(pe, q_split, g)
                    wait(pe, k_split, g)
                    scores(b, t, range(0, NS // 2))
                if runs(b, t, 0):
                    if t == 0:
                        pe.wait_ge(ln.n_ready, b + 1)
                        if cross:
                            pe.wait_ge(c_ready, b + 1)
                    if t % 2:
                        wait(pe, v_copied, KB * (5 * b + t // 2 + 1))
                    elif t == 8 and not is_last(b):
                        pe.wait_ge(ln.n32_ready, b + 2)
                    else:
                        wait(pe, q_split, g)
                    for i, (ws, xs_, rows) in enumerate(N_TERMS):
                        last = mm(pa[:, 0:SQ], wq[0:rows, ws, t * P:(t + 1) * P], nt[0:rows, xs_, :],
                                  start=i == 0, stop=i == len(N_TERMS) - 1)
                    last.then_inc(q_ready, 1)
                    wait(pe, k_split, g)
                    for i, (ws, xs_, rows) in enumerate(K_TERMS):
                        last = mm(pb[:, 0:NK], wk[0:rows, ws, t * P:(t + 1) * P], (ct if cross else nt)[0:rows, xs_, :],
                                  start=i == 0, stop=i == len(K_TERMS) - 1)
                    last.then_inc(k_ready, 1)
                if runs(b, t, 1):
                    scores(b, t, range(NS // 2, NS))
                if runs(b, t, 0) and t % 2 == 0:
                    pe.wait_ge(q_split, g + 1)
                    values(b, t, 0)
                if runs(b, t, 0) and t == 7 and not is_last(b):
                    pe.wait_ge(q_split, g + 1)
                    ln.pe_transpose(pe, b + 1)
                if runs(b, t, 3):
                    g3, par, p = g - 3, (t - 3) % 2, (t - 3) % PAIRS
                    wait(pe, ot_ready, g3)
                    wait(pe, sum_ready, 2 * (g3 + 1))
                    for h in range(2):
                        mm(pv[h * D1:(h + 1) * D1, SQ:2 * SQ], ones[:], key_sum[:, par, h, :], start=True, stop=True)
                    for kt in range(KT):
                        for h in range(2):
                            c0 = p * P + h * D1
                            last = mm(pv[h * D1:(h + 1) * D1, 0:SQ], v[:, kt, c0:c0 + D1], probs[:, par, h, kt, :],
                                      start=kt == 0, stop=kt == KT - 1)
                    last.then_inc(pv_done, 1)
                if runs(b, t, 0) and t % 2 == 0 and cross:
                    pe.wait_ge(k_split, g + 1)
                    values(b, t, 1)
                if runs(b, t, 4):
                    g4, par, p = g - 4, t % 2, (t - 4) % PAIRS
                    if p == 0:
                        wait(pe, y_taken, b)
                    wait(pe, ot_ready, g4 + 1)
                    for qt in range(QT):
                        last = mm(py[:, qt * C:(qt + 1) * C], ot[:, par, qt * P:(qt + 1) * P], wo[:, p, :],
                                  start=p == 0 and qt == 0, stop=p == PAIRS - 1, skip_group_check=True)
                    last.then_inc(y_acc, 1)

            pe.wait_ge(ones_set, 1)
            pe.wait_ge(zeroed, 1)
            pe.wait_ge(small_in, 48)
            ln.pe_transpose(pe, 0)
            pe.wait_ge(w_done, len(pieces))
            over_batches(pe, lambda b: [step(b, t) for t in range(PAIRS)])
            tail(step)

        @block.scalar
        def _(act):
            def hi_ctx(m):
                act.wait_ge(ctx_in, 16 * (m + 1))
                nc.scalar.activation(ct[:, 0:2], ct32[:], ACT.Copy).then_inc(c_hi, 1)

            def step(b, t):
                g = PAIRS * b + t
                if runs(b, t, 2):
                    g2, par = g - 2, t % 2
                    wait(act, pv_done, g2 - 1)
                    for h in range(2):
                        for kb in range(KB):
                            n = h * KB + kb
                            act.wait_ge(st_ready, NB * g2 + n + 1)
                            nc.scalar.activation(probs[:, par, h, 2 * kb:2 * kb + 2, :],
                                                 pst[:, n % 2, :].rearrange("p (k q) -> p k q", k=2),
                                                 ACT.Exp, scale=SCALE).then_inc(exp_done, 1)
                if runs(b, t, 0):
                    par = t % 2
                    act.wait_ge(q_ready, g + 1)
                    nc.scalar.activation(qh[:, par, :], pa[:, 0:SQ], ACT.Copy).then_inc(q_hi, 1)
                    act.wait_ge(k_ready, g + 1)
                    for h in range(2):
                        half = slice(h * D1, (h + 1) * D1)
                        last = nc.scalar.activation(kh[half, par, h, :], pb[half, 0:NK], ACT.Copy)
                    last.then_inc(k_hi, 1)
                    if t % 2 == 0:
                        for kb in range(KB):
                            act.wait_ge(v_ready, KB * (5 * b + t // 2) + kb + 1)
                            nc.scalar.activation(v[:, 2 * kb:2 * kb + 2, t * P:t * P + 256],
                                                 (pa, pb)[kb][:].rearrange("p (k c) -> p k c", k=2),
                                                 ACT.Copy).then_inc(v_copied, 1)
                    if t == PAIRS - 1 and not is_last(b):
                        ln.act_hi(act, b + 1)
                        if cross:
                            hi_ctx(b + 1)

            high_w(act)
            ln.act_hi(act, 0)
            if cross:
                hi_ctx(0)
            over_batches(act, lambda b: [step(b, t) for t in range(PAIRS)])
            tail(step)

        @block.vector
        def _(dve):
            def lo_ctx(m):
                dve.wait_ge(c_hi, m + 1)
                nc.vector.tensor_tensor(ct[:, 2:4], ct32[:], ct[:, 0:2].bitcast(FP32),
                                        ALU.subtract).then_inc(c_ready, 1)

            def maxima(b, t, which):
                g1, par = PAIRS * b + t - 1, (t - 1) % 2
                for i in which:
                    dve.wait_ge(score_ready, NS * g1 + i + 1)
                    if cross:
                        h, qt = i // QT, i % QT
                        out, src = negmax[:, par, h, qt:qt + 1], pscore[:, i % 2, :]
                    else:
                        out, src = negmax[:, par, i, :], pscore[:, i % 2, :].rearrange("p (q k) -> p q k", q=QT)
                    nc.vector.tensor_reduce(out, src, AX.X, ALU.max, negate=True).then_inc(max_done, 1)

            def step(b, t):
                g = PAIRS * b + t
                if runs(b, t, 1):
                    maxima(b, t, range(0, NS // 2))
                if runs(b, t, 0):
                    par = t % 2
                    dve.wait_ge(q_hi, g + 1)
                    nc.vector.tensor_tensor(ql[:, par, :], pa[:, 0:SQ], qh[:, par, :].bitcast(FP32),
                                            ALU.subtract).then_inc(q_split, 1)
                    dve.wait_ge(k_hi, g + 1)
                    for h in range(2):
                        half = slice(h * D1, (h + 1) * D1)
                        last = nc.vector.tensor_tensor(kl[half, par, h, :], pb[half, 0:NK],
                                                       kh[half, par, h, :].bitcast(FP32), ALU.subtract)
                    last.then_inc(k_split, 1)
                if runs(b, t, 1):
                    maxima(b, t, range(NS // 2, NS))
                if runs(b, t, 3):
                    g3, par = g - 3, (t - 3) % 2
                    dve.wait_ge(pv_done, g3 + 1)
                    nc.vector.reciprocal(recip[:], pv[:, SQ:2 * SQ]).then_inc(recip_done, 1)
                    dve.wait_ge(recip_done, g3 + 1)
                    wait(dve, y_acc, g3 - 1)
                    nc.vector.tensor_tensor(ot[:, par, :], pv[:, 0:SQ], recip[:], ALU.mult).then_inc(ot_ready, 1)
                if runs(b, t, 4) and t % PAIRS == 3:
                    m = b - 1 if t < PAIRS else b
                    dve.wait_ge(y_acc, g - 3)
                    dve.wait_ge(ln.biased, m + 1)
                    nc.vector.tensor_tensor(xs[:, m], xs[:, m], py[:, 0:QT * C].rearrange("p (q c) -> p q c", q=QT),
                                            ALU.add).then_inc(y_taken, 1)
                if runs(b, t, 0) and not is_last(b):
                    if t == 5:
                        ln.dve_stats(dve, b + 1)
                    if t == 6:
                        ln.dve_xhat(dve, b + 1)
                    if t == 7:
                        ln.dve_n32(dve, b + 1)
                    if t == PAIRS - 1:
                        ln.dve_lo(dve, b + 1)
                        if cross:
                            lo_ctx(b + 1)

            nc.vector.memset(ones[:], 1.0)
            nc.vector.memset(ones_b[:], 1.0).then_inc(ones_set, 1)
            dve.wait_ge(small_in, 48)
            ln.dve_stats(dve, 0)
            ln.dve_xhat(dve, 0)
            ln.dve_n32(dve, 0)
            low_w(dve)
            ln.dve_lo(dve, 0)
            if cross:
                lo_ctx(0)
            over_batches(dve, lambda b: [step(b, t) for t in range(PAIRS)])
            tail(step)

        @block.gpsimd
        def _(pool):
            def key_sums(b, t, h):
                g2, par = PAIRS * b + t - 2, t % 2
                if h == 0:
                    wait(pool, pv_done, g2 - 1)
                pool.wait_ge(exp_done, NB * g2 + (h + 1) * KB)
                src = probs[:, par, h]
                if cross:
                    nc.gpsimd.tensor_tensor(half_sum[:, par, h], src[:, 0:2], src[:, 2:4], ALU.add).then_inc(half_done, 1)
                    wait(pool, half_done, 2 * g2 + h + 1)
                    src = half_sum[:, par, h]
                nc.gpsimd.tensor_tensor(key_sum[:, par, h], src[:, 0], src[:, 1], ALU.add).then_inc(sum_ready, 1)

            def on_diagonal(out, values):
                n = values.shape[-1]
                nc.gpsimd.tensor_tensor(out.rearrange("p (n c) -> p n c", n=n),
                                        ident.unsqueeze(1).broadcast_to([P, n, P]),
                                        values.unsqueeze(2).broadcast_to([P, n, P]), ALU.mult).then_inc(diag_ready, 1)

            def diagonals(b, t, h):
                g1, par = PAIRS * b + t - 1, (t - 1) % 2
                if h == 0:
                    wait(pool, exp_done, NB * (g1 - 1))
                pool.wait_ge(max_done, NS * g1 + (h + 1) * NS // 2)
                on_diagonal(diag[:, par, h, :], negmax[:, par, h, :])

            def step(b, t):
                for h in range(2):
                    if runs(b, t, 2):
                        key_sums(b, t, h)
                    if runs(b, t, 1):
                        diagonals(b, t, h)
                if runs(b, t, 0) and t == 5 and not is_last(b):
                    ln.pool_rstd(pool, b + 1)

            nc.gpsimd.memset(kh[:].bitcast(FP32), 0.0)
            last = nc.gpsimd.memset(kl[:].bitcast(FP32), 0.0)
            last.then_inc(zeroed, 1)
            ln.pool_setup(pool)
            ln.pool_rstd(pool, 0)
            over_batches(pool, lambda b: [step(b, t) for t in range(PAIRS)])
            tail(step)


GROUP = 4
GROUPS = HEADS // GROUP
ROWS = P // GROUP


def narrow_attention_layer(nc, tag, xs, ident, dram, x_t, ctx_t):
    KT = SK // P
    NB = GROUP * KT // 2
    NS = GROUP * QT
    STEPS = 2 * GROUPS
    TURNS = B // 2
    SCALE = float(D0) ** -0.5
    total = GROUPS * B
    WIDE = GROUPS * P

    with ExitStack() as ctx:
        sb = lambda name, shape, dt: ctx.enter_context(nc.sbuf_tensor(f"{tag}_{name}", shape, dt))
        ps = lambda name, shape: ctx.enter_context(nc.psum_tensor(f"{tag}_{name}", shape, FP32))
        sem = lambda name: ctx.enter_context(nc.semaphore(f"{tag}_{name}"))

        wq = sb("wq", [P, 3, WIDE], FP32R)
        wk = sb("wk", [P, 4, WIDE], FP32R)
        wk_ip = sb("wk_ip", [P, 4, WIDE], FP32R)
        wv = sb("wv", [P, 4, 2 * C], FP32R)
        wo = sb("wo", [P, GROUPS, C], FP32)
        bo_rows = sb("bo_rows", [P, QT, C], FP32)
        staging = sb("staging", [P, 2, WIDE], FP32)
        marks = sb("marks", [P, 12], FP32)
        q_lo, q_sign, k_lo, k_sign = (marks[:, i:i + 1] for i in range(4))
        head_mask = [marks[:, 4 + j:5 + j] for j in range(GROUP)]
        is_text, is_ip = marks[:, 8:9], marks[:, 9:10]
        part = sb("part", [P, 2, P], BF16)
        part32 = sb("part32", [P, 2, P], FP32)
        pick = sb("pick", [P, P], FP32)
        ones_b = sb("ones_b", [P, P], BF16)
        x32 = sb("x32", [P, 2, SQ], FP32)
        nt = sb("nt", [P, 3, SQ], FP32R)
        ct32 = sb("ct32", [P, 2, SK], FP32)
        ct = sb("ct", [P, 4, SK], FP32R)
        q_signed = sb("q_signed", [P, SQ], FP32R)
        k_signed = sb("k_signed", [P, SK], FP32R)
        q4 = sb("q4", [P, SQ], FP32)
        qm = sb("qm", [P, 2, GROUP, SQ], FP32R)
        k4 = sb("k4", [P, 2, SK], FP32R)
        v = sb("v", [P, 2, KT, HEADS, ROWS], FP32)
        negmax = sb("negmax", [P, 2, GROUP, 2, QT], FP32)
        diag = sb("diag", [P, 2, GROUP, 2, SQ], BF16)
        probs = sb("probs", [P, 2, GROUP, KT, SQ], FP32)
        sums = sb("sums", [P, 2, SQ], FP32)
        recip = sb("recip", [P, SQ], FP32)
        ot = sb("ot", [P, GROUPS, SQ], FP32)
        pa, pb, pv, pd = ps("pa", [P, 512]), ps("pb", [P, 512]), ps("pv", [P, 512]), ps("pd", [P, 512])
        pscore = ps("pscore", [P, 2, 512])
        pst = ps("pst", [P, 2, 512])

        loaded = [sem("loaded0"), sem("loaded1")]
        rounded, w_done, small_in = sem("rounded"), sem("w_done"), sem("small_in")
        v_cleared, v_marked, consts_set = sem("v_cleared"), sem("v_marked"), sem("consts_set")
        x_in, ctx_in, in_hi, in_ready = sem("x_in"), sem("ctx_in"), sem("in_hi"), sem("in_ready")
        qk_ready, a_rounded, b_rounded = sem("qk_ready"), sem("a_rounded"), sem("b_rounded")
        q4_done, qm_ready, k4_ready = sem("q4_done"), sem("qm_ready"), sem("k4_ready")
        v_ready, v_copied = sem("v_ready"), sem("v_copied")
        score_ready, max_done, diag_ready = sem("score_ready"), sem("max_done"), sem("diag_ready")
        st_ready, exp_done = sem("st_ready"), sem("exp_done")
        pv_done, sums_copied, den_ready = sem("pv_done"), sem("sums_copied"), sem("den_ready")
        recip_done, ot_ready = sem("recip_done"), sem("ot_ready")
        biased, y_ready, y_taken = sem("biased"), sem("y_ready"), sem("y_taken")

        pieces = n_weight_pieces(dram["wq"], dram["wq_ext"], wq)
        for w, src in ((wk, dram["wk"]), (wk_ip, dram["wk_ip"]), (wv, dram["wv"])):
            for half in range(2):
                pieces.append((src[half], P, w[:, half, :], w[:, 2 + half, :], (0, P)))
        load_w, high_w, low_w = split_weights(nc, (loaded, rounded, w_done), staging, pieces)

        def runs(a, t, lag):
            return not isinstance(a, int) or 0 <= STEPS * a + t - lag < total

        def turns(eng, step, lags):
            for t in range(STEPS):
                step(0, t)
            with eng.Fori(1, TURNS - 1) as a:
                for t in range(STEPS):
                    step(a, t)
            for t in range(STEPS + lags):
                step(TURNS - 1, t)

        def next_batch(a, t):
            if t % GROUPS != GROUPS - 1 or (isinstance(a, int) and STEPS * a + t >= total - 1):
                return None
            return 2 * a + t // GROUPS + 1

        block = ctx.enter_context(nc.Block())

        @block.sync
        def _(sp):
            for place, name in ((marks, "marks"), (part32, "part"), (pick, "pick"), (wo, "wo"), (bo_rows, "bo_rows")):
                sp.dma_start(place[:], dram[name]).then_inc(small_in, 16)
            sp.dma_start(x32[:], x_t[0]).then_inc(x_in, 16)
            sp.dma_start(ct32[:], ctx_t[0]).then_inc(ctx_in, 16)
            load_w(sp)
            with sp.Fori(1, B) as b:
                sp.wait_ge(in_ready, b)
                sp.dma_start(x32[:], x_t[b]).then_inc(x_in, 16)
                sp.dma_start(ct32[:], ctx_t[b]).then_inc(ctx_in, 16)

        @block.tensor
        def _(pe):
            mm = nc.tensor.matmul

            def scores(a, t, which):
                g1, par = STEPS * a + t - 1, (t - 1) % 2
                for i in which:
                    wait(pe, max_done, NS * g1 + i - 1)
                    j, qt = i // QT, i % QT
                    mm(pscore[:, i % 2, :], qm[:, par, j, qt * P:(qt + 1) * P], k4[:, par, :],
                       start=True, stop=True).then_inc(score_ready, 1)

            def project(out, w, rows_cols, acts, terms):
                for i, (ws, xs_, rows) in enumerate(terms):
                    last = mm(out, w[0:rows, ws, rows_cols], acts(xs_, rows), start=i == 0, stop=i == len(terms) - 1)
                return last

            def step(a, t):
                g = STEPS * a + t
                u = t % GROUPS
                if runs(a, t, 2):
                    g2, par = g - 2, t % 2
                    wait(pe, diag_ready, GROUP * (g2 + 1))
                    for j in range(GROUP):
                        for kb in range(KT // 2):
                            n = j * (KT // 2) + kb
                            wait(pe, exp_done, NB * g2 + n - 1)
                            for i in range(2):
                                kt = 2 * kb + i
                                out = pst[:, n % 2, i * SQ:(i + 1) * SQ]
                                if kt == 0:
                                    mm(out, part[:, 0, :], diag[:, par, j, 0, :], start=True, stop=False)
                                mm(out, part[:, 1, :] if kt == 0 else ones_b[:], diag[:, par, j, 1, :],
                                   start=kt > 0, stop=False)
                                last = mm(out, k4[:, par, kt * P:(kt + 1) * P], qm[:, par, j, :], start=False, stop=True)
                            last.then_inc(st_ready, 1)
                if runs(a, t, 1):
                    wait(pe, qm_ready, g)
                    wait(pe, k4_ready, g)
                    scores(a, t, range(0, 3))
                if runs(a, t, 0):
                    b = 2 * a + t // GROUPS
                    if u == 0:
                        pe.wait_ge(in_ready, b + 1)
                    if u == 3:
                        pe.wait_ge(v_copied, KT * (b + 1))
                    else:
                        wait(pe, q4_done, g)
                        wait(pe, k4_ready, g)
                    cols = slice(u * P, (u + 1) * P)
                    project(pa[:, 0:SQ], wq, cols, lambda s, r: nt[0:r, s, :], N_TERMS)
                    project(pa[:, SQ:2 * SQ], wk, cols, lambda s, r: ct[0:r, s, 0:SQ], CTX_TERMS)
                    project(pb[:], wk_ip, cols, lambda s, r: ct[0:r, s, :], CTX_TERMS).then_inc(qk_ready, 1)
                if runs(a, t, 1):
                    scores(a, t, range(3, 6))
                if runs(a, t, 3):
                    g3, par, u3 = g - 3, (t - 3) % 2, (t - 3) % GROUPS
                    vb = (t - 3) // GROUPS % 2
                    if u3 == 0:
                        wait(pe, v_copied, KT * ((2 * a + t // GROUPS if t < STEPS else B - 1) + 1))
                    wait(pe, sums_copied, g3)
                    wait(pe, exp_done, NB * (g3 + 1))
                    for kt in range(KT):
                        for j in range(GROUP):
                            last = mm(pv[j * ROWS:(j + 1) * ROWS, 0:SQ], v[:, vb, kt, GROUP * u3 + j, :],
                                      probs[:, par, j, kt, :], start=kt == 0, stop=kt == KT - 1)
                    last.then_inc(pv_done, 1)
                if runs(a, t, 1):
                    scores(a, t, range(6, NS))
                if runs(a, t, 5) and (t - 5) % GROUPS == GROUPS - 1:
                    wait(pe, ot_ready, g - 4)
                    for qt in range(QT):
                        for u5 in range(GROUPS):
                            last = mm(pd[:, qt * C:(qt + 1) * C], ot[:, u5, qt * P:(qt + 1) * P], wo[:, u5, :],
                                      start=u5 == 0, stop=u5 == GROUPS - 1)
                    last.then_inc(y_ready, 1)
                if runs(a, t, 4):
                    g4, par = g - 4, t % 2
                    if (t - 4) % GROUPS == 0:
                        wait(pe, y_taken, 2 * a + (t - 4) // GROUPS)
                    else:
                        wait(pe, ot_ready, g4)
                    wait(pe, sums_copied, g4 + 1)
                    mm(pd[:, 0:SQ], pick[:], sums[:, par, :], start=True, stop=True).then_inc(den_ready, 1)
                if runs(a, t, 0) and u == 2:
                    b = 2 * a + t // GROUPS
                    pe.wait_ge(q4_done, g + 1)
                    pe.wait_ge(k4_ready, g + 1)
                    for kt in range(KT):
                        if kt >= 2:
                            pe.wait_ge(v_copied, KT * b + kt - 1)
                        for i, (ws, xs_, rows) in enumerate(CTX_TERMS):
                            last = mm((pa, pb)[kt % 2][:, 0:2 * C], ct[0:rows, xs_, kt * P:(kt + 1) * P],
                                      wv[0:rows, ws, :], start=i == 0, stop=i == len(CTX_TERMS) - 1)
                        last.then_inc(v_ready, 1)

            pe.wait_ge(consts_set, 1)
            pe.wait_ge(small_in, 80)
            pe.wait_ge(w_done, len(pieces))
            turns(pe, step, 6)

        @block.scalar
        def _(act):
            def hi_inputs(m):
                act.wait_ge(x_in, 16 * (m + 1))
                nc.scalar.activation(nt[:, 0], x32[:, 0], ACT.Copy)
                nc.scalar.activation(nt[0:EXT, 2], x32[0:EXT, 1], ACT.Copy)
                act.wait_ge(ctx_in, 16 * (m + 1))
                nc.scalar.activation(ct[:, 0:2], ct32[:], ACT.Copy).then_inc(in_hi, 1)

            def step(a, t):
                g = STEPS * a + t
                u = t % GROUPS
                if runs(a, t, 2):
                    g2, par = g - 2, t % 2
                    wait(act, pv_done, g2 - 1)
                    for j in range(GROUP):
                        for kb in range(KT // 2):
                            n = j * (KT // 2) + kb
                            act.wait_ge(st_ready, NB * g2 + n + 1)
                            nc.scalar.activation(probs[:, par, j, 2 * kb:2 * kb + 2, :],
                                                 pst[:, n % 2, :].rearrange("p (k q) -> p k q", k=2),
                                                 ACT.Exp, scale=SCALE).then_inc(exp_done, 1)
                if runs(a, t, 0):
                    par = t % 2
                    act.wait_ge(qk_ready, g + 1)
                    nc.scalar.activation(q_signed[:], pa[:, 0:SQ], ACT.Copy, scale=q_sign)
                    nc.scalar.activation(k_signed[:, 0:TEXT], pa[:, SQ:SQ + TEXT], ACT.Copy,
                                         scale=k_sign).then_inc(a_rounded, 1)
                    nc.scalar.activation(k_signed[:, TEXT:SK], pb[:, TEXT:SK], ACT.Copy,
                                         scale=k_sign).then_inc(b_rounded, 1)
                    act.wait_ge(q4_done, g + 1)
                    for j in range(GROUP):
                        last = nc.scalar.activation(qm[:, par, j, :], q4[:], ACT.Copy, scale=head_mask[j])
                    last.then_inc(qm_ready, 1)
                if runs(a, t, 3):
                    g3, par = g - 3, (t - 3) % 2
                    act.wait_ge(pv_done, g3 + 1)
                    wait(act, ot_ready, g3 - 1)
                    nc.scalar.activation(sums[:, par, :], pv[:, 0:SQ], ACT.Copy).then_inc(sums_copied, 1)
                if runs(a, t, 0) and u == 2:
                    b, vb = 2 * a + t // GROUPS, t // GROUPS
                    for kt in range(KT):
                        act.wait_ge(v_ready, KT * b + kt + 1)
                        src = (pa, pb)[kt % 2]
                        heads = lambda i: src[:, i * C:(i + 1) * C].rearrange("p (h d) -> p h d", d=D0)
                        ip = v[:, vb, kt, :, D0:2 * D0]
                        if kt == 0:
                            nc.scalar.activation(v[:, vb, 0, :, 0:D0], heads(0), ACT.Copy, scale=is_text)
                            last = nc.scalar.activation(ip, heads(1), ACT.Copy, scale=is_ip)
                        else:
                            last = nc.scalar.activation(ip, heads(1), ACT.Copy)
                        last.then_inc(v_copied, 1)
                if (m := next_batch(a, t)) is not None:
                    hi_inputs(m)

            act.wait_ge(small_in, 80)
            act.wait_ge(v_marked, 1)
            hi_inputs(0)
            high_w(act)
            turns(act, step, 6)

        @block.vector
        def _(dve):
            def lo_inputs(m):
                dve.wait_ge(in_hi, m + 1)
                minus = lambda out, x, hi: nc.vector.tensor_tensor(out, x, hi.bitcast(FP32), ALU.subtract)
                minus(nt[:, 1], x32[:, 0], nt[:, 0])
                minus(nt[2 * REST:EXT, 2], x32[2 * REST:EXT, 1], nt[2 * REST:EXT, 2])
                minus(ct[:, 2:4], ct32[:], ct[:, 0:2]).then_inc(in_ready, 1)

            def maxima(a, t, which):
                g1, par = STEPS * a + t - 1, (t - 1) % 2
                for i in which:
                    dve.wait_ge(score_ready, NS * g1 + i + 1)
                    j, qt = i // QT, i % QT
                    for s, keys in enumerate((slice(0, TEXT), slice(TEXT, SK))):
                        last = nc.vector.tensor_reduce(negmax[:, par, j, s, qt:qt + 1], pscore[:, i % 2, keys],
                                                       AX.X, ALU.max, negate=True)
                    last.then_inc(max_done, 1)

            def step(a, t):
                g = STEPS * a + t
                if runs(a, t, 1):
                    maxima(a, t, range(0, 3))
                if runs(a, t, 0):
                    par = t % 2
                    fuse = nc.vector.scalar_tensor_tensor
                    dve.wait_ge(a_rounded, g + 1)
                    fuse(out=q4[:], in0=pa[:, 0:SQ], scalar=q_lo, in1=q_signed[:].bitcast(FP32),
                         op0=ALU.mult, op1=ALU.add)
                    fuse(out=k4[:, par, 0:TEXT], in0=pa[:, SQ:SQ + TEXT], scalar=k_lo,
                         in1=k_signed[:, 0:TEXT].bitcast(FP32), op0=ALU.mult, op1=ALU.add).then_inc(q4_done, 1)
                    dve.wait_ge(b_rounded, g + 1)
                    fuse(out=k4[:, par, TEXT:SK], in0=pb[:, TEXT:SK], scalar=k_lo,
                         in1=k_signed[:, TEXT:SK].bitcast(FP32), op0=ALU.mult, op1=ALU.add).then_inc(k4_ready, 1)
                if runs(a, t, 1):
                    maxima(a, t, range(3, NS))
                if runs(a, t, 5) and (t - 5) % GROUPS == GROUPS - 1:
                    m = 2 * a + (t - 5) // GROUPS
                    nc.vector.tensor_tensor(xs[:, m], xs[:, m], bo_rows[:], ALU.add).then_inc(biased, 1)
                    dve.wait_ge(biased, m + 1)
                    dve.wait_ge(y_ready, m + 1)
                    nc.vector.tensor_tensor(xs[:, m], xs[:, m], pd[:, 0:QT * C].rearrange("p (q c) -> p q c", q=QT),
                                            ALU.add).then_inc(y_taken, 1)
                if runs(a, t, 4):
                    g4, par, u4 = g - 4, t % 2, (t - 4) % GROUPS
                    dve.wait_ge(den_ready, g4 + 1)
                    nc.vector.reciprocal(recip[:], pd[:, 0:SQ]).then_inc(recip_done, 1)
                    dve.wait_ge(recip_done, g4 + 1)
                    nc.vector.tensor_tensor(ot[:, u4, :], sums[:, par, :], recip[:], ALU.mult).then_inc(ot_ready, 1)
                if next_batch(a, t) is not None:
                    lo_inputs(next_batch(a, t))

            nc.vector.memset(ones_b[:], 1.0)
            dve.wait_ge(small_in, 80)
            nc.vector.tensor_copy(part[:], part32[:]).then_inc(consts_set, 1)
            dve.wait_ge(v_cleared, 1)
            for vb in range(2):
                nc.vector.memset(v[:, vb, 1:KT, :, 3 * D0:4 * D0], 1.0)
                for s in range(2):
                    cols = slice((2 + s) * D0, (3 + s) * D0)
                    last = nc.vector.tensor_scalar(v[:, vb, 0, :, cols], v[:, vb, 0, :, cols],
                                                   marks[:, 8 + s:9 + s], None, ALU.add)
            last.then_inc(v_marked, 1)
            lo_inputs(0)
            low_w(dve)
            turns(dve, step, 6)

        @block.gpsimd
        def _(pool):
            def step(a, t):
                if runs(a, t, 1):
                    g1, par = STEPS * a + t - 1, (t - 1) % 2
                    wait(pool, exp_done, NB * (g1 - 1))
                    for j in range(GROUP):
                        pool.wait_ge(max_done, NS * g1 + QT * (j + 1))
                        nc.gpsimd.tensor_tensor(diag[:, par, j].rearrange("p s (q c) -> p (s q) c", q=QT),
                                                ident.unsqueeze(1).broadcast_to([P, 2 * QT, P]),
                                                negmax[:, par, j].rearrange("p s q -> p (s q)").unsqueeze(2)
                                                .broadcast_to([P, 2 * QT, P]), ALU.mult).then_inc(diag_ready, 1)

            nc.gpsimd.memset(v[:], 0.0).then_inc(v_cleared, 1)
            turns(pool, step, 6)


def feed_forward_layer(nc, tag, xs, ident, dram, out):
    FT = FF // P

    with ExitStack() as ctx:
        sb = lambda name, shape, dt: ctx.enter_context(nc.sbuf_tensor(f"{tag}_{name}", shape, dt))
        ps = lambda name, shape: ctx.enter_context(nc.psum_tensor(f"{tag}_{name}", shape, FP32))
        sem = lambda name: ctx.enter_context(nc.semaphore(f"{tag}_{name}"))

        w1 = sb("w1", [P, 3, 2 * FF], FP32R)
        w2 = sb("w2", [P, FT, C], FP32)
        b1 = sb("b1", [P, 2 * FT], FP32)
        b2_rows = sb("b2_rows", [P, QT, C], FP32)
        gains = sb("gains", [P, 4], FP32)
        staging = sb("staging", [P, 2, 2 * FF], FP32)
        nt = sb("nt", [P, 3, SQ], FP32R)
        gate = sb("gate", [P, FT, SQ], FP32)
        hidden = sb("hidden", [P, FT, SQ], FP32)
        ph = ps("ph", [P, FT, 512])
        pt, py = ps("pt", [P, 512]), ps("py", [P, 512])

        loaded = [sem("loaded0"), sem("loaded1")]
        rounded, w_done, small_in = sem("rounded"), sem("w_done"), sem("small_in")
        h_ready, gelu_done, hidden_ready = sem("h_ready"), sem("gelu_done"), sem("hidden_ready")
        y_ready, y_taken, stored = sem("y_ready"), sem("y_taken"), sem("stored")

        ln = LayerNorm(nc, ctx, f"{tag}_ln", xs, ident, nt, gains, b2_rows[:], pt)
        pieces = n_weight_pieces(dram["w1"], dram["w1_ext"], w1)
        load_w, high_w, low_w = split_weights(nc, (loaded, rounded, w_done), staging, pieces)
        block = ctx.enter_context(nc.Block())

        @block.sync
        def _(sp):
            for place, name in ((gains, "gains"), (b2_rows, "b2_rows"), (b1, "b1"), (w2, "w2")):
                sp.dma_start(place[:], dram[name]).then_inc(small_in, 16)
            load_w(sp)
            with sp.Fori(0, B) as b:
                sp.wait_ge(y_taken, b + 1)
                sp.dma_start(out[b], xs[:, b]).then_inc(stored, 16)
            sp.wait_ge(stored, 16 * B)

        @block.tensor
        def _(pe):
            mm = nc.tensor.matmul

            def batch(b):
                pe.wait_ge(ln.n_ready, b + 1)
                for i in range(FT):
                    wait(pe, hidden_ready, FT * (b - 1) + i + 1)
                    for s in range(2):
                        cols = slice((s * FT + i) * P, (s * FT + i + 1) * P)
                        for k, (ws, xs_, rows) in enumerate(N_TERMS):
                            last = mm(ph[:, i, s * SQ:(s + 1) * SQ], w1[0:rows, ws, cols], nt[0:rows, xs_, :],
                                      start=k == 0, stop=k == len(N_TERMS) - 1)
                    last.then_inc(h_ready, 1)
                if not is_last(b):
                    ln.pe_transpose(pe, b + 1)
                wait(pe, y_taken, b)
                for qt in range(QT):
                    for i in range(FT):
                        pe.wait_ge(hidden_ready, FT * b + i + 1)
                        last = mm(py[:, qt * C:(qt + 1) * C], hidden[:, i, qt * P:(qt + 1) * P], w2[:, i, :],
                                  start=i == 0, stop=i == FT - 1)
                last.then_inc(y_ready, 1)

            pe.wait_ge(small_in, 64)
            ln.pe_transpose(pe, 0)
            pe.wait_ge(w_done, len(pieces))
            over_batches(pe, batch)

        @block.scalar
        def _(act):
            def batch(b):
                for i in range(FT):
                    act.wait_ge(h_ready, FT * b + i + 1)
                    nc.scalar.activation(gate[:, i, :], ph[:, i, SQ:2 * SQ], ACT.Gelu,
                                         bias=b1[:, FT + i:FT + i + 1]).then_inc(gelu_done, 1)
                if not is_last(b):
                    ln.act_hi(act, b + 1)

            high_w(act)
            act.wait_ge(small_in, 64)
            ln.act_hi(act, 0)
            over_batches(act, batch)

        @block.vector
        def _(dve):
            def batch(b):
                if not is_last(b):
                    ln.dve_stats(dve, b + 1)
                    ln.dve_xhat(dve, b + 1)
                for i in range(FT):
                    dve.wait_ge(gelu_done, FT * b + i + 1)
                    nc.vector.scalar_tensor_tensor(out=hidden[:, i, :], in0=ph[:, i, 0:SQ], scalar=b1[:, i:i + 1],
                                                   in1=gate[:, i, :], op0=ALU.add,
                                                   op1=ALU.mult).then_inc(hidden_ready, 1)
                if not is_last(b):
                    ln.dve_n32(dve, b + 1)
                    ln.dve_lo(dve, b + 1)
                dve.wait_ge(y_ready, b + 1)
                dve.wait_ge(ln.biased, b + 1)
                nc.vector.tensor_tensor(xs[:, b], xs[:, b], py[:, 0:QT * C].rearrange("p (q c) -> p q c", q=QT),
                                        ALU.add).then_inc(y_taken, 1)

            dve.wait_ge(small_in, 64)
            ln.dve_stats(dve, 0)
            ln.dve_xhat(dve, 0)
            ln.dve_n32(dve, 0)
            low_w(dve)
            ln.dve_lo(dve, 0)
            over_batches(dve, batch)

        @block.gpsimd
        def _(pool):
            ln.pool_setup(pool)
            ln.pool_rstd(pool, 0)
            with pool.Fori(1, B) as b:
                ln.pool_rstd(pool, b)


def build(nc, t, out):
    with ExitStack() as ctx:
        xs = ctx.enter_context(nc.sbuf_tensor("xs", [P, B, QT, C], FP32))
        ident = ctx.enter_context(nc.sbuf_tensor("identity", [P, P], FP32))
        inputs_in = ctx.enter_context(nc.semaphore("inputs_in"))
        with nc.Block() as block:
            @block.sync
            def _(sp):
                sp.dma_start(ident[:], t["ident"]).then_inc(inputs_in, 16)
                with sp.Fori(0, B) as b:
                    sp.dma_start(xs[:, b], t["x"][b]).then_inc(inputs_in, 16)
                sp.wait_ge(inputs_in, 16 * (B + 1))
        narrow_attention_layer(nc, "l0", xs, ident[:], t["l0"], t["x_t"], t["ctx_t"])
        attention_layer(nc, "a1", xs, ident[:], t["a1"], None)
        attention_layer(nc, "a2", xs, ident[:], t["a2"], t["ctx_t"])
        feed_forward_layer(nc, "ff", xs, ident[:], t["ff"], out)


def laid_out(inputs):
    x, ctx = inputs["x"], inputs["ctx_2048"]
    halves = lambda w: w.reshape(2, P, w.shape[-1])
    main = lambda w: w[:P]
    ext = lambda w: np.concatenate([w[P:]] * 3)
    rows = lambda bias: np.broadcast_to(bias, (P, QT, C))
    by_tile = lambda w: w.reshape(-1, P, w.shape[-1]).transpose(1, 0, 2)

    arrays = {"ident": np.eye(P, dtype=np.float32),
              "x": x.reshape(B, QT, P, C).transpose(0, 2, 1, 3),
              "ctx_t": ctx.transpose(0, 2, 1).reshape(B, 2, P, SK).transpose(0, 2, 1, 3)}
    x_t = x.transpose(0, 2, 1)
    both = np.zeros((B, P, 2, SQ), np.float32)
    both[:, :, 0] = x_t[:, :P]
    both[:, :EXT, 1] = np.concatenate([x_t[:, P:]] * 3, axis=1)
    arrays["x_t"] = both

    repeat = lambda w: np.broadcast_to(w.reshape(-1, HEADS, 1, D0), (w.shape[0], HEADS, 4, D0)).reshape(w.shape[0], -1)
    w0 = {k: inputs[f"L0_xattn_{k}"].T for k in ("Wq", "Wk", "Wv", "Wk_ip", "Wv_ip", "Wo")}
    wq = repeat(w0["Wq"])
    marks = np.zeros((P, 12), np.float32)
    r = np.arange(P) % ROWS // D0
    marks[:, 0], marks[:, 1] = r % 2, 1 - 2 * (r % 2)
    marks[:, 2], marks[:, 3] = r // 2, 1 - 2 * (r // 2)
    for j in range(GROUP):
        marks[j * ROWS:(j + 1) * ROWS, 4 + j] = 1
    marks[:TEXT, 8] = 1
    marks[TEXT:, 9] = 1
    part = np.zeros((P, 2, P), np.float32)
    part[:, 0, :TEXT] = 1
    part[:, 1, TEXT:] = 1
    pick = np.zeros((P, P), np.float32)
    m = np.arange(P)
    pick[np.where(m % ROWS < 2 * D0, m + 2 * D0, m), m] = 1
    wo = np.zeros((GROUPS, GROUP, 4, D0, C), np.float32)
    wo[:, :, 0] = wo[:, :, 1] = w0["Wo"].reshape(GROUPS, GROUP, D0, C)
    layers = {"l0": {"wq": main(wq), "wq_ext": ext(wq), "wk": halves(repeat(w0["Wk"])),
                     "wk_ip": halves(repeat(w0["Wk_ip"])),
                     "wv": halves(np.concatenate([w0["Wv"], w0["Wv_ip"]], axis=1)),
                     "wo": wo.reshape(GROUPS, P, C).transpose(1, 0, 2), "bo_rows": rows(inputs["L0_xattn_bo"]),
                     "marks": marks, "part": part, "pick": pick}}

    def gains(n):
        g, b = inputs[f"L1_xattn_{n}_g"], inputs[f"L1_xattn_{n}_b"]
        out = np.zeros((P, 4), np.float32)
        out[:, 0], out[:, 1] = g[:P], b[:P]
        out[:EXT, 2], out[:EXT, 3] = np.concatenate([g[P:]] * 3), np.concatenate([b[P:]] * 3)
        return out

    for a, n in (("a1", "ln1"), ("a2", "ln2")):
        w = {k: inputs[f"L1_xattn_{a}_{k}"] for k in ("wq", "wk", "wv", "wo", "bo")}
        layers[a] = {"wq": main(w["wq"]), "wq_ext": ext(w["wq"]), "wo": by_tile(w["wo"]),
                     "bo_rows": rows(w["bo"]), "gains": gains(n)}
        for k in ("wk", "wv"):
            if a == "a1":
                layers[a] |= {k: main(w[k]), k + "_ext": ext(w[k])}
            else:
                layers[a][k] = halves(w[k])
    w1 = inputs["L1_xattn_ff_w1"]
    layers["ff"] = {"w1": main(w1), "w1_ext": ext(w1), "w2": by_tile(inputs["L1_xattn_ff_w2"]),
                    "b1": inputs["L1_xattn_ff_b1"].reshape(-1, P).T, "b2_rows": rows(inputs["L1_xattn_ff_b2"]),
                    "gains": gains("ln3")}
    for layer, named in layers.items():
        arrays |= {f"{layer}.{name}": a for name, a in named.items()}
    return arrays


def kernel(**inputs):
    from concourse import bacc
    from concourse.bass_utils import run_bass_kernel_spmd

    inputs = {k: np.asarray(v) for k, v in inputs.items()}
    arrays = {f"in_{k.replace('.', '_')}": np.ascontiguousarray(a) for k, a in laid_out(inputs).items()}
    nc = bacc.Bacc("TRN2", target_bir_lowering=False, num_devices=1)
    t = {}
    for key in laid_out(inputs):
        name = f"in_{key.replace('.', '_')}"
        a = arrays[name]
        ap = nc.dram_tensor(name, a.shape, mybir.dt.from_np(a.dtype), kind="ExternalInput").ap()
        if "." in key:
            layer, part = key.split(".")
            t.setdefault(layer, {})[part] = ap
        else:
            t[key] = ap
    out = nc.dram_tensor("out", (B, P, QT, C), FP32, kind="ExternalOutput").ap()
    build(nc, t, out)
    r = run_bass_kernel_spmd(nc, [arrays], core_ids=[0])
    return r.results[0]["out"].transpose(0, 2, 1, 3).reshape(B, SQ, C)
```

```python
import numpy as np
import concourse.bass as bass
from concourse import mybir
from contextlib import ExitStack

FP32 = mybir.dt.float32
FP32R = mybir.dt.float32r
BF16 = mybir.dt.bfloat16
ALU = mybir.AluOpType
ACT = mybir.ActivationFunctionType
AX = mybir.AxisListType

B, SQ, C = 8, 256, 160
SK, CC = 512, 256
TEXT = 77
HEADS = 20
D0 = C // HEADS
D1 = 64
INNER = HEADS * D1
FF = 4 * C
P = 128
QT = SQ // P
REST = C - P
EXT = 3 * REST
PAIRS = HEADS // 2
EPS = 1e-5

N_TERMS = [(0, 0, P), (1, 0, P), (0, 1, P), (2, 2, EXT)]
CTX_TERMS = [(0, 0, P), (1, 1, P), (2, 0, P), (3, 1, P), (0, 2, P), (1, 3, P)]


def wait(eng, sem, value):
    if isinstance(value, int) and value <= 0:
        return
    eng.wait_ge(sem, value)


def over_batches(eng, body):
    body(0)
    with eng.Fori(1, B - 1) as b:
        body(b)
    body(B - 1)


def is_last(b):
    return isinstance(b, int) and b == B - 1


def split_weights(nc, sems, staging, pieces):
    loaded, rounded, done = sems

    def load(sp):
        for k, (src, rows, _, _, _) in enumerate(pieces):
            wait(sp, done, k - 1)
            sp.dma_start(staging[0:rows, k % 2, 0:src.shape[1]], src).then_inc(loaded[k % 2], 16)

    def high(act):
        for k, (src, rows, hi, _, _) in enumerate(pieces):
            act.wait_ge(loaded[k % 2], 16 * (k // 2 + 1))
            nc.scalar.activation(hi, staging[0:rows, k % 2, 0:src.shape[1]], ACT.Copy).then_inc(rounded, 1)

    def low(dve):
        for k, (src, rows, hi, lo, lo_rows) in enumerate(pieces):
            r0, r1 = lo_rows
            dve.wait_ge(rounded, k + 1)
            minus = lo if lo_rows != (0, rows) else hi
            nc.vector.tensor_tensor(lo, staging[r0:r1, k % 2, 0:src.shape[1]], minus.bitcast(FP32),
                                    ALU.subtract).then_inc(done, 1)

    return load, high, low


def n_weight_pieces(src_main, src_ext, slots):
    return [(src_main, P, slots[:, 0, :], slots[:, 1, :], (0, P)),
            (src_ext, EXT, slots[0:EXT, 2, :], slots[REST:2 * REST, 2, :], (REST, 2 * REST))]


class LayerNorm:

    def __init__(self, nc, ctx, tag, xs, ident, n_terms, gains, bias_rows, psum):
        sb = lambda name, shape, dt: ctx.enter_context(nc.sbuf_tensor(f"{tag}_{name}", shape, dt))
        sem = lambda name: ctx.enter_context(nc.semaphore(f"{tag}_{name}"))
        self.nc, self.xs, self.ident, self.nt, self.gains, self.rows, self.psum = (
            nc, xs, ident, n_terms, gains, bias_rows, psum)
        self.stats = sb("stats", [P, QT, 6], FP32)
        self.mv = sb("mv", [P, QT, 2], FP32)
        self.var = sb("var", [P, QT], FP32)
        self.aggregated = sb("aggregated", [P, 1], FP32)
        self.rstd = sb("rstd", [P, QT], FP32)
        self.half = sb("half", [P, QT], FP32)
        self.xhat = sb("xhat", [P, QT, P + EXT], FP32)
        self.n32 = sb("n32", [P, 2, SQ], FP32)
        self.half_set = sem("half_set")
        self.stats_chain = sem("stats_chain")
        self.var_ready = sem("var_ready")
        self.rstd_ready = sem("rstd_ready")
        self.xhat_ready = sem("xhat_ready")
        self.biased = sem("biased")
        self.t_ready = sem("t_ready")
        self.n32_ready = sem("n32_ready")
        self.n_hi = sem("n_hi")
        self.n_ready = sem("n_ready")

    def pool_setup(self, pool):
        self.nc.gpsimd.memset(self.half[:], -0.5).then_inc(self.half_set, 1)
        pool.wait_ge(self.half_set, 1)

    def dve_stats(self, dve, m):
        nc = self.nc
        for qt in range(QT):
            last = nc.vector.bn_stats(self.stats[:, qt], self.xs[:, m, qt])
        last.then_inc(self.stats_chain, 1)
        wait(dve, self.stats_chain, 2 * m + 1)
        nc.vector.memset(self.aggregated[:], 0.0)
        for qt in range(QT):
            last = nc.vector.bn_aggr(self.mv[:, qt], self.stats[:, qt])
        last.then_inc(self.stats_chain, 1)
        wait(dve, self.stats_chain, 2 * m + 2)
        nc.vector.tensor_scalar(self.var[:], self.mv[:, :, 1], EPS, None, ALU.add).then_inc(self.var_ready, 1)

    def pool_rstd(self, pool, m):
        pool.wait_ge(self.var_ready, m + 1)
        self.nc.gpsimd.tensor_tensor(self.rstd[:], self.var[:], self.half[:], ALU.pow).then_inc(self.rstd_ready, 1)

    def dve_xhat(self, dve, m):
        nc = self.nc
        dve.wait_ge(self.rstd_ready, m + 1)
        for qt in range(QT):
            scalars = (self.mv[:, qt, 0:1], self.rstd[:, qt:qt + 1])
            nc.vector.tensor_scalar(self.xhat[:, qt, 0:C], self.xs[:, m, qt], *scalars, ALU.subtract, ALU.mult)
            for r in range(1, 3):
                last = nc.vector.tensor_scalar(self.xhat[:, qt, P + r * REST:P + (r + 1) * REST],
                                               self.xs[:, m, qt, P:C], *scalars, ALU.subtract, ALU.mult)
        last.then_inc(self.xhat_ready, 1)
        dve.wait_ge(self.xhat_ready, m + 1)
        nc.vector.tensor_tensor(self.xs[:, m], self.xs[:, m], self.rows, ALU.add).then_inc(self.biased, 1)

    def pe_transpose(self, pe, m):
        nc = self.nc
        pe.wait_ge(self.xhat_ready, m + 1)
        for qt in range(QT):
            nc.tensor.transpose(self.psum[:, qt * P:(qt + 1) * P], self.xhat[:, qt, 0:P], self.ident)
        for qt in range(QT):
            last = nc.tensor.transpose(self.psum[0:EXT, SQ + qt * P:SQ + (qt + 1) * P],
                                       self.xhat[:, qt, P:P + EXT], self.ident)
        last.then_inc(self.t_ready, 1)

    def dve_n32(self, dve, m):
        nc = self.nc
        dve.wait_ge(self.t_ready, m + 1)
        g, gains = self.gains, nc.vector.tensor_scalar
        gains(self.n32[:, 0], self.psum[:, 0:SQ], g[:, 0:1], g[:, 1:2], ALU.mult, ALU.add)
        gains(self.n32[0:EXT, 1], self.psum[0:EXT, SQ:2 * SQ], g[0:EXT, 2:3], g[0:EXT, 3:4],
              ALU.mult, ALU.add).then_inc(self.n32_ready, 1)

    def act_hi(self, act, m):
        nc = self.nc
        act.wait_ge(self.n32_ready, m + 1)
        nc.scalar.activation(self.nt[:, 0], self.n32[:, 0], ACT.Copy)
        nc.scalar.activation(self.nt[0:EXT, 2], self.n32[0:EXT, 1], ACT.Copy).then_inc(self.n_hi, 1)

    def dve_lo(self, dve, m):
        nc = self.nc
        dve.wait_ge(self.n_hi, m + 1)
        nc.vector.tensor_tensor(self.nt[:, 1], self.n32[:, 0], self.nt[:, 0].bitcast(FP32), ALU.subtract)
        lo = self.nt[2 * REST:EXT, 2]
        nc.vector.tensor_tensor(lo, self.n32[2 * REST:EXT, 1], lo.bitcast(FP32),
                                ALU.subtract).then_inc(self.n_ready, 1)


def attention_layer(nc, tag, xs, ident, dram, ctx_t):
    cross = ctx_t is not None
    NK = SK if cross else SQ
    KT = NK // P
    KB = KT // 2
    NB = 2 * KB
    NS = 2 * QT if cross else 2
    KSLOTS = 4 if cross else 3
    K_TERMS = CTX_TERMS if cross else N_TERMS
    SCALE = float(D1) ** -0.5
    total = PAIRS * B

    with ExitStack() as ctx:
        sb = lambda name, shape, dt: ctx.enter_context(nc.sbuf_tensor(f"{tag}_{name}", shape, dt))
        ps = lambda name, shape: ctx.enter_context(nc.psum_tensor(f"{tag}_{name}", shape, FP32))
        sem = lambda name: ctx.enter_context(nc.semaphore(f"{tag}_{name}"))

        wq = sb("wq", [P, 3, INNER], FP32R)
        wk = sb("wk", [P, KSLOTS, INNER], FP32R)
        wv = sb("wv", [P, KSLOTS, INNER], FP32R)
        wo = sb("wo", [P, PAIRS, C], FP32)
        gains = sb("gains", [P, 4], FP32)
        bo_rows = sb("bo_rows", [P, QT, C], FP32)
        staging = sb("staging", [P, 2, INNER], FP32)
        ones = sb("ones", [P, D1], FP32)
        nt = sb("nt", [P, 3, SQ], FP32R)
        q1 = sb("q1", [P, 2, 2, SQ], FP32R)
        k1 = sb("k1", [P, 2, 2, NK], FP32R)
        q2 = sb("q2", [P, 2, 2, SQ], FP32R)
        k2 = sb("k2", [P, 2, 2, NK], FP32R)
        v = sb("v", [P, KT, INNER], FP32)
        negmax = sb("negmax", [P, 2, QT, 2], FP32)
        probs = sb("probs", [P, 2, 2, KT, SQ], FP32)
        half_sum = sb("half_sum", [P, 2, 2, 2, SQ], FP32)
        key_sum = sb("key_sum", [P, 2, 2, SQ], FP32)
        recip = sb("recip", [P, SQ], FP32)
        ot = sb("ot", [P, PAIRS, SQ], FP32)
        if cross:
            ct32 = sb("ct32", [P, 2, NK], FP32)
            ct = sb("ct", [P, 4, NK], FP32R)
        pa, pb, pv = ps("pa", [P, 512]), ps("pb", [P, 512]), ps("pv", [P, 2, 512])
        pscore = ps("pscore", [P, 2, 512])
        pst = ps("pst", [P, 2, 512])

        loaded = [sem("loaded0"), sem("loaded1")]
        rounded, w_done, small_in = sem("rounded"), sem("w_done"), sem("small_in")
        zeroed, ones_set = sem("zeroed"), sem("ones_set")
        ctx_in, c_hi, c_ready = sem("ctx_in"), sem("c_hi"), sem("c_ready")
        q_ready, q_hi, q_split = sem("q_ready"), sem("q_hi"), sem("q_split")
        k_ready, k_hi, k_split = sem("k_ready"), sem("k_hi"), sem("k_split")
        v_ready, v_copied = sem("v_ready"), sem("v_copied")
        score_ready, max_done = sem("score_ready"), sem("max_done")
        max_turned, max_placed, rows_set = sem("max_turned"), sem("max_placed"), sem("rows_set")
        st_ready, exp_done = sem("st_ready"), sem("exp_done")
        half_done, sum_ready = sem("half_done"), sem("sum_ready")
        pv_done, recip_done, ot_ready = sem("pv_done"), sem("recip_done"), sem("ot_ready")
        y_ready, y_taken = sem("y_ready"), sem("y_taken")

        ln = LayerNorm(nc, ctx, f"{tag}_ln", xs, ident, nt, gains, bo_rows[:], pa)
        pieces = n_weight_pieces(dram["wq"], dram["wq_ext"], wq)
        if cross:
            for w, src in ((wk, dram["wk"]), (wv, dram["wv"])):
                for half in range(2):
                    pieces.append((src[half], P, w[:, half, :], w[:, 2 + half, :], (0, P)))
        else:
            pieces += n_weight_pieces(dram["wk"], dram["wk_ext"], wk)
            pieces += n_weight_pieces(dram["wv"], dram["wv_ext"], wv)
        load_w, high_w, low_w = split_weights(nc, (loaded, rounded, w_done), staging, pieces)

        def runs(b, t, lag):
            return not isinstance(b, int) or 0 <= PAIRS * b + t - lag < total

        def tail(body):
            for t in range(PAIRS, PAIRS + 7):
                body(B - 1, t)

        own = [slice(h * D1, (h + 1) * D1) for h in range(2)]
        other = [slice((1 - h) * D1, (2 - h) * D1) for h in range(2)]
        extra = [slice((1 - h) * D1, (1 - h) * D1 + 2) for h in range(2)]

        block = ctx.enter_context(nc.Block())

        @block.sync
        def _(sp):
            sp.dma_start(gains[:], dram["gains"]).then_inc(small_in, 16)
            sp.dma_start(bo_rows[:], dram["bo_rows"]).then_inc(small_in, 16)
            sp.dma_start(wo[:], dram["wo"]).then_inc(small_in, 16)
            if cross:
                sp.dma_start(ct32[:], ctx_t[0]).then_inc(ctx_in, 16)
            load_w(sp)
            if cross:
                with sp.Fori(1, B) as b:
                    sp.wait_ge(c_ready, b)
                    sp.dma_start(ct32[:], ctx_t[b]).then_inc(ctx_in, 16)

        @block.tensor
        def _(pe):
            mm = nc.tensor.matmul

            def scores(b, t, which):
                g1, par = PAIRS * b + t - 1, (t - 1) % 2
                for i in which:
                    n = NS * g1 + i
                    wait(pe, max_done, n - 1)
                    if cross:
                        last = mm(pscore[:, i % 2, :], q1[:, par, i // QT, (i % QT) * P:(i % QT + 1) * P],
                                  k1[:, par, i // QT, :], start=True, stop=True)
                    else:
                        for qt in range(QT):
                            last = mm(pscore[:, i % 2, qt * NK:(qt + 1) * NK], q1[:, par, i, qt * P:(qt + 1) * P],
                                      k1[:, par, i, :], start=True, stop=True)
                    last.then_inc(score_ready, 1)

            def values(b, t, kb):
                bank = (pa, pb)[kb]
                acts = ct if cross else nt
                for j in range(2):
                    kt = 2 * kb + j
                    for i, (ws, xs_, rows) in enumerate(K_TERMS):
                        last = mm(bank[:, j * 256:(j + 1) * 256], acts[0:rows, xs_, kt * P:(kt + 1) * P],
                                  wv[0:rows, ws, t * P:t * P + 256], start=i == 0, stop=i == len(K_TERMS) - 1)
                last.then_inc(v_ready, 1)

            def keys(t):
                for i, (ws, xs_, rows) in enumerate(K_TERMS):
                    last = mm(pb[:, 0:NK], wk[0:rows, ws, t * P:(t + 1) * P], (ct if cross else nt)[0:rows, xs_, :],
                              start=i == 0, stop=i == len(K_TERMS) - 1)
                last.then_inc(k_ready, 1)

            def turned_scores(b, t, n):
                g2, par, h, kb = PAIRS * b + t - 2, t % 2, n // KB, n % KB
                wait(pe, exp_done, NB * g2 + n - 1)
                for j in range(2):
                    out = pst[:, n % 2, j * SQ:(j + 1) * SQ]
                    kt = slice((2 * kb + j) * P, (2 * kb + j + 1) * P)
                    mm(out, k1[:, par, h, kt], q1[:, par, h, :], start=True, stop=False)
                    last = mm(out, k2[:, par, h, kt], q2[:, par, h, :], start=False, stop=True)
                last.then_inc(st_ready, 1)

            def step(b, t):
                g = PAIRS * b + t
                if runs(b, t, 2):
                    wait(pe, max_placed, g - 1)
                for n in range(NB):
                    if runs(b, t, 2):
                        turned_scores(b, t, n)
                    if n == 0 and runs(b, t, 1):
                        wait(pe, q_split, g)
                        wait(pe, k_split, g)
                    if runs(b, t, 1):
                        scores(b, t, range(n, n + 1))
                if runs(b, t, 0):
                    if t == 0:
                        pe.wait_ge(ln.n_ready, b + 1)
                        if cross:
                            pe.wait_ge(c_ready, b + 1)
                    wait(pe, q_split, g)
                    wait(pe, k_split, g)
                    if t == 8 and not is_last(b):
                        pe.wait_ge(ln.n32_ready, b + 2)
                    if t == 6:
                        wait(pe, y_taken, 2 * b)
                    if t == 0:
                        wait(pe, y_taken, 2 * b - 1)
                    if t % 2 == 0:
                        for kb in range(KB):
                            values(b, t, kb)
                    if not cross:
                        keys(t)
                    if t % 2 == 0:
                        pe.wait_ge(v_copied, KB * (5 * b + t // 2 + 1))
                    for i, (ws, xs_, rows) in enumerate(N_TERMS):
                        last = mm(pa[:, 0:SQ], wq[0:rows, ws, t * P:(t + 1) * P], nt[0:rows, xs_, :],
                                  start=i == 0, stop=i == len(N_TERMS) - 1)
                    last.then_inc(q_ready, 1)
                    if cross:
                        keys(t)
                if runs(b, t, 1):
                    g1, par = g - 1, (t - 1) % 2
                    wait(pe, max_done, NS * (g1 + 1))
                    for qt in range(QT):
                        last = nc.tensor.transpose(pscore[0:2, 0, qt * P:(qt + 1) * P], negmax[:, par, qt, :], ident)
                    last.then_inc(max_turned, 1)
                if runs(b, t, 3):
                    g3, par, p = g - 3, (t - 3) % 2, (t - 3) % PAIRS
                    wait(pe, ot_ready, g3 - 1)
                    wait(pe, sum_ready, 2 * (g3 + 1))
                    for h in range(2):
                        mm(pv[own[h], par, SQ:2 * SQ], ones[:], key_sum[:, par, h, :], start=True, stop=True)
                    for kt in range(KT):
                        for h in range(2):
                            c0 = p * P + h * D1
                            last = mm(pv[own[h], par, 0:SQ], v[:, kt, c0:c0 + D1], probs[:, par, h, kt, :],
                                      start=kt == 0, stop=kt == KT - 1)
                    last.then_inc(pv_done, 1)
                if runs(b, t, 0) and t == 7 and not is_last(b):
                    pe.wait_ge(q_split, g + 1)
                    ln.pe_transpose(pe, b + 1)
                if t % PAIRS in (5, 9) and runs(b, t, 6):
                    if runs(b, t, 0):
                        pe.wait_ge(q_split, g + 1)
                    pe.wait_ge(ot_ready, g - (5 if t % PAIRS == 5 else 4))
                    first = 5 if t % PAIRS == 5 else 0
                    for qt in range(QT):
                        for p in range(first, first + 5):
                            last = mm(pa[:, qt * C:(qt + 1) * C], ot[:, p, qt * P:(qt + 1) * P], wo[:, p, :],
                                      start=p == first, stop=p == first + 4)
                    last.then_inc(y_ready, 1)

            pe.wait_ge(ones_set, 1)
            pe.wait_ge(rows_set, 1)
            pe.wait_ge(small_in, 48)
            ln.pe_transpose(pe, 0)
            pe.wait_ge(w_done, len(pieces))
            over_batches(pe, lambda b: [step(b, t) for t in range(PAIRS)])
            tail(step)

        @block.scalar
        def _(act):
            def hi_ctx(m):
                act.wait_ge(ctx_in, 16 * (m + 1))
                nc.scalar.activation(ct[:, 0:2], ct32[:], ACT.Copy).then_inc(c_hi, 1)

            def step(b, t):
                g = PAIRS * b + t
                if runs(b, t, 2):
                    g2, par = g - 2, t % 2
                    wait(act, pv_done, g2 - 1)
                    for h in range(2):
                        for kb in range(KB):
                            n = h * KB + kb
                            act.wait_ge(st_ready, NB * g2 + n + 1)
                            nc.scalar.activation(probs[:, par, h, 2 * kb:2 * kb + 2, :],
                                                 pst[:, n % 2, :].rearrange("p (k q) -> p k q", k=2),
                                                 ACT.Exp, scale=SCALE).then_inc(exp_done, 1)
                if runs(b, t, 0):
                    par = t % 2
                    if t % 2 == 0:
                        for kb in range(KB):
                            act.wait_ge(v_ready, KB * (5 * b + t // 2) + kb + 1)
                            nc.scalar.activation(v[:, 2 * kb:2 * kb + 2, t * P:t * P + 256],
                                                 (pa, pb)[kb][:].rearrange("p (k c) -> p k c", k=2),
                                                 ACT.Copy).then_inc(v_copied, 1)
                    act.wait_ge(q_ready, g + 1)
                    for h in range(2):
                        nc.scalar.activation(q1[own[h], par, h, :], pa[own[h], 0:SQ], ACT.Copy)
                        nc.scalar.activation(q1[other[h], par, h, :], pa[own[h], 0:SQ], ACT.Copy).then_inc(q_hi, 1)
                if runs(b, t, 1):
                    act.wait_ge(max_turned, g)
                    for h in range(2):
                        last = nc.scalar.activation(q2[extra[h], (t - 1) % 2, h, :], pscore[0:2, 0, 0:SQ], ACT.Copy)
                    last.then_inc(max_placed, 1)
                if runs(b, t, 0):
                    act.wait_ge(k_ready, g + 1)
                    for h in range(2):
                        nc.scalar.activation(k1[own[h], par, h, :], pb[own[h], 0:NK], ACT.Copy)
                        nc.scalar.activation(k2[own[h], par, h, :], pb[own[h], 0:NK], ACT.Copy).then_inc(k_hi, 1)
                    if t == PAIRS - 1 and not is_last(b):
                        ln.act_hi(act, b + 1)
                        if cross:
                            hi_ctx(b + 1)

            act.wait_ge(zeroed, 1)
            for par in range(2):
                for h in range(2):
                    last = nc.scalar.activation(k2[extra[h], par, h, :], ident[0:2, h:h + 1].broadcast_to([2, NK]),
                                                ACT.Copy)
            last.then_inc(rows_set, 1)
            high_w(act)
            ln.act_hi(act, 0)
            if cross:
                hi_ctx(0)
            over_batches(act, lambda b: [step(b, t) for t in range(PAIRS)])
            tail(step)

        @block.vector
        def _(dve):
            def lo_ctx(m):
                dve.wait_ge(c_hi, m + 1)
                nc.vector.tensor_tensor(ct[:, 2:4], ct32[:], ct[:, 0:2].bitcast(FP32),
                                        ALU.subtract).then_inc(c_ready, 1)

            def maxima(b, t, which):
                g1, par = PAIRS * b + t - 1, (t - 1) % 2
                for i in which:
                    dve.wait_ge(score_ready, NS * g1 + i + 1)
                    if cross:
                        h, qt = i // QT, i % QT
                        out, src = negmax[:, par, qt, h:h + 1], pscore[:, i % 2, :]
                    else:
                        out, src = negmax[:, par, :, i], pscore[:, i % 2, :].rearrange("p (q k) -> p q k", q=QT)
                    nc.vector.tensor_reduce(out, src, AX.X, ALU.max, negate=True).then_inc(max_done, 1)

            def step(b, t):
                g = PAIRS * b + t
                if runs(b, t, 0) and t == 8 and not is_last(b):
                    ln.dve_n32(dve, b + 1)
                if t % PAIRS in (0, 6) and runs(b, t, 7):
                    m = b - 1 if t < PAIRS else b
                    dve.wait_ge(y_ready, 2 * m + (1 if t % PAIRS == 0 else 2))
                    dve.wait_ge(ln.biased, m + 1)
                    nc.vector.tensor_tensor(xs[:, m], xs[:, m], pa[:, 0:QT * C].rearrange("p (q c) -> p q c", q=QT),
                                            ALU.add).then_inc(y_taken, 1)
                if runs(b, t, 1):
                    maxima(b, t, range(NS))
                if runs(b, t, 4):
                    g4, par, p = g - 4, t % 2, (t - 4) % PAIRS
                    wait(dve, ot_ready, g4)
                    dve.wait_ge(pv_done, g4 + 1)
                    nc.vector.reciprocal(recip[:], pv[:, par, SQ:2 * SQ]).then_inc(recip_done, 1)
                    dve.wait_ge(recip_done, g4 + 1)
                    nc.vector.tensor_tensor(ot[:, p, :], pv[:, par, 0:SQ], recip[:], ALU.mult).then_inc(ot_ready, 1)
                if runs(b, t, 0):
                    par = t % 2
                    dve.wait_ge(q_hi, 2 * (g + 1))
                    for h in range(2):
                        last = nc.vector.tensor_tensor(q2[own[h], par, h, :], pa[own[h], 0:SQ],
                                                       q1[own[h], par, h, :].bitcast(FP32), ALU.subtract)
                    last.then_inc(q_split, 1)
                    for h in range(2):
                        dve.wait_ge(k_hi, 2 * g + h + 1)
                        last = nc.vector.tensor_tensor(k1[other[h], par, h, :], pb[own[h], 0:NK],
                                                       k2[own[h], par, h, :].bitcast(FP32), ALU.subtract)
                    last.then_inc(k_split, 1)
                if runs(b, t, 0) and not is_last(b):
                    if t == 5:
                        ln.dve_stats(dve, b + 1)
                    if t == 6:
                        ln.dve_xhat(dve, b + 1)
                    if t == PAIRS - 1:
                        ln.dve_lo(dve, b + 1)
                        if cross:
                            lo_ctx(b + 1)

            nc.vector.memset(ones[:], 1.0).then_inc(ones_set, 1)
            dve.wait_ge(small_in, 48)
            ln.dve_stats(dve, 0)
            ln.dve_xhat(dve, 0)
            ln.dve_n32(dve, 0)
            low_w(dve)
            ln.dve_lo(dve, 0)
            if cross:
                lo_ctx(0)
            over_batches(dve, lambda b: [step(b, t) for t in range(PAIRS)])
            tail(step)

        @block.gpsimd
        def _(pool):
            def key_sums(b, t, h):
                g2, par = PAIRS * b + t - 2, t % 2
                if h == 0:
                    wait(pool, pv_done, g2 - 1)
                pool.wait_ge(exp_done, NB * g2 + (h + 1) * KB)
                src = probs[:, par, h]
                if cross:
                    nc.gpsimd.tensor_tensor(half_sum[:, par, h], src[:, 0:2], src[:, 2:4], ALU.add).then_inc(half_done, 1)
                    wait(pool, half_done, 2 * g2 + h + 1)
                    src = half_sum[:, par, h]
                nc.gpsimd.tensor_tensor(key_sum[:, par, h], src[:, 0], src[:, 1], ALU.add).then_inc(sum_ready, 1)

            def step(b, t):
                for h in range(2):
                    if runs(b, t, 2):
                        key_sums(b, t, h)
                if runs(b, t, 0) and t == 5 and not is_last(b):
                    ln.pool_rstd(pool, b + 1)

            nc.gpsimd.memset(q2[:].bitcast(FP32), 0.0)
            nc.gpsimd.memset(k2[:].bitcast(FP32), 0.0).then_inc(zeroed, 1)
            ln.pool_setup(pool)
            ln.pool_rstd(pool, 0)
            over_batches(pool, lambda b: [step(b, t) for t in range(PAIRS)])
            tail(step)


GROUP = 4
GROUPS = HEADS // GROUP
ROWS = P // GROUP


def narrow_attention_layer(nc, tag, xs, ident, dram, x_t, ctx_t):
    KT = SK // P
    NB = GROUP * KT // 2
    NS = GROUP * QT
    STEPS = 2 * GROUPS
    TURNS = B // 2
    SCALE = float(D0) ** -0.5
    total = GROUPS * B
    WIDE = GROUPS * P

    with ExitStack() as ctx:
        sb = lambda name, shape, dt: ctx.enter_context(nc.sbuf_tensor(f"{tag}_{name}", shape, dt))
        ps = lambda name, shape: ctx.enter_context(nc.psum_tensor(f"{tag}_{name}", shape, FP32))
        sem = lambda name: ctx.enter_context(nc.semaphore(f"{tag}_{name}"))

        wq = sb("wq", [P, 3, WIDE], FP32R)
        wk = sb("wk", [P, 4, WIDE], FP32R)
        wk_ip = sb("wk_ip", [P, 4, WIDE], FP32R)
        wv = sb("wv", [P, 4, 2 * C], FP32R)
        wo = sb("wo", [P, GROUPS, C], FP32)
        bo_rows = sb("bo_rows", [P, QT, C], FP32)
        staging = sb("staging", [P, 2, WIDE], FP32)
        marks = sb("marks", [P, 12], FP32)
        q_lo, q_sign, k_lo, k_sign = (marks[:, i:i + 1] for i in range(4))
        head_mask = [marks[:, 4 + j:5 + j] for j in range(GROUP)]
        is_text, is_ip = marks[:, 8:9], marks[:, 9:10]
        part = sb("part", [P, 2, P], BF16)
        part32 = sb("part32", [P, 2, P], FP32)
        pick = sb("pick", [P, P], FP32)
        ones_b = sb("ones_b", [P, P], BF16)
        x32 = sb("x32", [P, 2, SQ], FP32)
        nt = sb("nt", [P, 3, SQ], FP32R)
        ct32 = sb("ct32", [P, 2, SK], FP32)
        ct = sb("ct", [P, 4, SK], FP32R)
        q_signed = sb("q_signed", [P, SQ], FP32R)
        k_signed = sb("k_signed", [P, SK], FP32R)
        q4 = sb("q4", [P, SQ], FP32)
        qm = sb("qm", [P, 2, GROUP, SQ], FP32R)
        k4 = sb("k4", [P, 2, SK], FP32R)
        v = sb("v", [P, 2, KT, HEADS, ROWS], FP32)
        negmax = sb("negmax", [P, 2, GROUP, 2, QT], FP32)
        diag = sb("diag", [P, 2, GROUP, 2, SQ], BF16)
        probs = sb("probs", [P, 2, GROUP, KT, SQ], FP32)
        sums = sb("sums", [P, 2, SQ], FP32)
        recip = sb("recip", [P, SQ], FP32)
        ot = sb("ot", [P, GROUPS, SQ], FP32)
        pa, pb, pv, pd = ps("pa", [P, 512]), ps("pb", [P, 512]), ps("pv", [P, 512]), ps("pd", [P, 512])
        pscore = ps("pscore", [P, 2, 512])
        pst = ps("pst", [P, 2, 512])

        loaded = [sem("loaded0"), sem("loaded1")]
        rounded, w_done, small_in = sem("rounded"), sem("w_done"), sem("small_in")
        v_cleared, v_marked, consts_set = sem("v_cleared"), sem("v_marked"), sem("consts_set")
        x_in, ctx_in, in_hi, in_ready = sem("x_in"), sem("ctx_in"), sem("in_hi"), sem("in_ready")
        q_ready, k_ready, a_rounded, b_rounded = sem("q_ready"), sem("k_ready"), sem("a_rounded"), sem("b_rounded")
        q4_done, qm_ready, k4_ready = sem("q4_done"), sem("qm_ready"), sem("k4_ready")
        v_ready, v_copied = sem("v_ready"), sem("v_copied")
        score_ready, max_done, diag_ready = sem("score_ready"), sem("max_done"), sem("diag_ready")
        st_ready, exp_done = sem("st_ready"), sem("exp_done")
        pv_done, sums_copied, den_ready = sem("pv_done"), sem("sums_copied"), sem("den_ready")
        recip_done, ot_ready = sem("recip_done"), sem("ot_ready")
        biased, y_ready, y_taken = sem("biased"), sem("y_ready"), sem("y_taken")

        pieces = n_weight_pieces(dram["wq"], dram["wq_ext"], wq)
        for w, src in ((wk, dram["wk"]), (wk_ip, dram["wk_ip"]), (wv, dram["wv"])):
            for half in range(2):
                pieces.append((src[half], P, w[:, half, :], w[:, 2 + half, :], (0, P)))
        load_w, high_w, low_w = split_weights(nc, (loaded, rounded, w_done), staging, pieces)

        def runs(a, t, lag):
            return not isinstance(a, int) or 0 <= STEPS * a + t - lag < total

        def turns(eng, step, lags):
            for t in range(STEPS):
                step(0, t)
            with eng.Fori(1, TURNS - 1) as a:
                for t in range(STEPS):
                    step(a, t)
            for t in range(STEPS + lags):
                step(TURNS - 1, t)

        def next_batch(a, t):
            if t % GROUPS != GROUPS - 1 or (isinstance(a, int) and STEPS * a + t >= total - 1):
                return None
            return 2 * a + t // GROUPS + 1

        block = ctx.enter_context(nc.Block())

        @block.sync
        def _(sp):
            for place, name in ((marks, "marks"), (part32, "part"), (pick, "pick"), (wo, "wo"), (bo_rows, "bo_rows")):
                sp.dma_start(place[:], dram[name]).then_inc(small_in, 16)
            sp.dma_start(x32[:], x_t[0]).then_inc(x_in, 16)
            sp.dma_start(ct32[:], ctx_t[0]).then_inc(ctx_in, 16)
            load_w(sp)
            with sp.Fori(1, B) as b:
                sp.wait_ge(in_ready, b)
                sp.dma_start(x32[:], x_t[b]).then_inc(x_in, 16)
                sp.dma_start(ct32[:], ctx_t[b]).then_inc(ctx_in, 16)

        @block.tensor
        def _(pe):
            mm = nc.tensor.matmul

            def scores(a, t, which):
                g1, par = STEPS * a + t - 1, (t - 1) % 2
                for i in which:
                    wait(pe, max_done, NS * g1 + i - 1)
                    j, qt = i // QT, i % QT
                    if qt == 0:
                        wait(pe, qm_ready, GROUP * g1 + j + 1)
                    mm(pscore[:, i % 2, :], qm[:, par, j, qt * P:(qt + 1) * P], k4[:, par, :],
                       start=True, stop=True).then_inc(score_ready, 1)

            def project(out, w, rows_cols, acts, terms):
                for i, (ws, xs_, rows) in enumerate(terms):
                    last = mm(out, w[0:rows, ws, rows_cols], acts(xs_, rows), start=i == 0, stop=i == len(terms) - 1)
                return last

            def turned_scores(a, t, n):
                g2, par, j, kb = STEPS * a + t - 2, t % 2, n // (KT // 2), n % (KT // 2)
                if kb == 0:
                    wait(pe, diag_ready, GROUP * g2 + j + 1)
                wait(pe, exp_done, NB * g2 + n - 1)
                for i in range(2):
                    kt = 2 * kb + i
                    out = pst[:, n % 2, i * SQ:(i + 1) * SQ]
                    if kt == 0:
                        mm(out, part[:, 0, :], diag[:, par, j, 0, :], start=True, stop=False)
                    mm(out, part[:, 1, :] if kt == 0 else ones_b[:], diag[:, par, j, 1, :],
                       start=kt > 0, stop=False)
                    last = mm(out, k4[:, par, kt * P:(kt + 1) * P], qm[:, par, j, :], start=False, stop=True)
                last.then_inc(st_ready, 1)

            def step(a, t):
                g = STEPS * a + t
                u = t % GROUPS
                if runs(a, t, 5) and (t - 5) % GROUPS == GROUPS - 1:
                    wait(pe, ot_ready, g - 4)
                    for qt in range(QT):
                        for u5 in range(GROUPS):
                            last = mm(pd[:, qt * C:(qt + 1) * C], ot[:, u5, qt * P:(qt + 1) * P], wo[:, u5, :],
                                      start=u5 == 0, stop=u5 == GROUPS - 1)
                    last.then_inc(y_ready, 1)
                for n in range(NB):
                    if runs(a, t, 2):
                        turned_scores(a, t, n)
                    if runs(a, t, 1):
                        if n == 0:
                            wait(pe, k4_ready, g)
                        scores(a, t, range(n, n + 1))
                    if n == 5 and runs(a, t, 4):
                        g4, par = g - 4, t % 2
                        if (t - 4) % GROUPS == 0:
                            wait(pe, y_taken, 2 * a + (t - 4) // GROUPS)
                        else:
                            wait(pe, ot_ready, g4)
                        wait(pe, sums_copied, g4 + 1)
                        mm(pd[:, 0:SQ], pick[:], sums[:, par, :], start=True, stop=True).then_inc(den_ready, 1)
                if runs(a, t, 0):
                    b = 2 * a + t // GROUPS
                    if u == 0:
                        pe.wait_ge(in_ready, b + 1)
                    if u == 3:
                        pe.wait_ge(v_copied, KT * (b + 1))
                    else:
                        wait(pe, q4_done, g)
                        wait(pe, k4_ready, g)
                    cols = slice(u * P, (u + 1) * P)
                    project(pa[:, 0:SQ], wq, cols, lambda s, r: nt[0:r, s, :], N_TERMS)
                    project(pa[:, SQ:2 * SQ], wk, cols, lambda s, r: ct[0:r, s, 0:SQ], CTX_TERMS).then_inc(q_ready, 1)
                    project(pb[:], wk_ip, cols, lambda s, r: ct[0:r, s, :], CTX_TERMS).then_inc(k_ready, 1)
                if runs(a, t, 3):
                    g3, par, u3 = g - 3, (t - 3) % 2, (t - 3) % GROUPS
                    vb = (t - 3) // GROUPS % 2
                    if u3 == 0:
                        wait(pe, v_copied, KT * ((2 * a + t // GROUPS if t < STEPS else B - 1) + 1))
                    wait(pe, sums_copied, g3)
                    wait(pe, exp_done, NB * (g3 + 1))
                    for kt in range(KT):
                        for j in range(GROUP):
                            last = mm(pv[j * ROWS:(j + 1) * ROWS, 0:SQ], v[:, vb, kt, GROUP * u3 + j, :],
                                      probs[:, par, j, kt, :], start=kt == 0, stop=kt == KT - 1)
                    last.then_inc(pv_done, 1)
                if runs(a, t, 0) and u == 2:
                    b = 2 * a + t // GROUPS
                    pe.wait_ge(q4_done, g + 1)
                    pe.wait_ge(k4_ready, g + 1)
                    for kt in range(KT):
                        if kt >= 2:
                            pe.wait_ge(v_copied, KT * b + kt - 1)
                        for i, (ws, xs_, rows) in enumerate(CTX_TERMS):
                            last = mm((pa, pb)[kt % 2][:, 0:2 * C], ct[0:rows, xs_, kt * P:(kt + 1) * P],
                                      wv[0:rows, ws, :], start=i == 0, stop=i == len(CTX_TERMS) - 1)
                        last.then_inc(v_ready, 1)

            pe.wait_ge(consts_set, 1)
            pe.wait_ge(small_in, 80)
            pe.wait_ge(w_done, len(pieces))
            turns(pe, step, 6)

        @block.scalar
        def _(act):
            def hi_inputs(m):
                act.wait_ge(x_in, 16 * (m + 1))
                nc.scalar.activation(nt[:, 0], x32[:, 0], ACT.Copy)
                nc.scalar.activation(nt[0:EXT, 2], x32[0:EXT, 1], ACT.Copy)
                act.wait_ge(ctx_in, 16 * (m + 1))
                nc.scalar.activation(ct[:, 0:2], ct32[:], ACT.Copy).then_inc(in_hi, 1)

            def step(a, t):
                g = STEPS * a + t
                u = t % GROUPS
                if runs(a, t, 2):
                    g2, par = g - 2, t % 2
                    wait(act, pv_done, g2 - 1)
                    for j in range(GROUP):
                        for kb in range(KT // 2):
                            n = j * (KT // 2) + kb
                            act.wait_ge(st_ready, NB * g2 + n + 1)
                            nc.scalar.activation(probs[:, par, j, 2 * kb:2 * kb + 2, :],
                                                 pst[:, n % 2, :].rearrange("p (k q) -> p k q", k=2),
                                                 ACT.Exp, scale=SCALE).then_inc(exp_done, 1)
                if runs(a, t, 0):
                    par = t % 2
                    act.wait_ge(q_ready, g + 1)
                    nc.scalar.activation(q_signed[:], pa[:, 0:SQ], ACT.Copy, scale=q_sign)
                    nc.scalar.activation(k_signed[:, 0:TEXT], pa[:, SQ:SQ + TEXT], ACT.Copy,
                                         scale=k_sign).then_inc(a_rounded, 1)
                    act.wait_ge(q4_done, g + 1)
                    for j in range(GROUP):
                        nc.scalar.activation(qm[:, par, j, :], q4[:], ACT.Copy,
                                             scale=head_mask[j]).then_inc(qm_ready, 1)
                    act.wait_ge(k_ready, g + 1)
                    nc.scalar.activation(k_signed[:, TEXT:SK], pb[:, TEXT:SK], ACT.Copy,
                                         scale=k_sign).then_inc(b_rounded, 1)
                if runs(a, t, 3):
                    g3, par = g - 3, (t - 3) % 2
                    act.wait_ge(pv_done, g3 + 1)
                    wait(act, ot_ready, g3 - 1)
                    nc.scalar.activation(sums[:, par, :], pv[:, 0:SQ], ACT.Copy).then_inc(sums_copied, 1)
                if runs(a, t, 0) and u == 2:
                    b, vb = 2 * a + t // GROUPS, t // GROUPS
                    for kt in range(KT):
                        act.wait_ge(v_ready, KT * b + kt + 1)
                        src = (pa, pb)[kt % 2]
                        heads = lambda i: src[:, i * C:(i + 1) * C].rearrange("p (h d) -> p h d", d=D0)
                        ip = v[:, vb, kt, :, D0:2 * D0]
                        if kt == 0:
                            nc.scalar.activation(v[:, vb, 0, :, 0:D0], heads(0), ACT.Copy, scale=is_text)
                            last = nc.scalar.activation(ip, heads(1), ACT.Copy, scale=is_ip)
                        else:
                            last = nc.scalar.activation(ip, heads(1), ACT.Copy)
                        last.then_inc(v_copied, 1)
                if (m := next_batch(a, t)) is not None:
                    hi_inputs(m)

            act.wait_ge(small_in, 80)
            act.wait_ge(v_marked, 1)
            hi_inputs(0)
            high_w(act)
            turns(act, step, 6)

        @block.vector
        def _(dve):
            def lo_inputs(m):
                dve.wait_ge(in_hi, m + 1)
                minus = lambda out, x, hi: nc.vector.tensor_tensor(out, x, hi.bitcast(FP32), ALU.subtract)
                minus(nt[:, 1], x32[:, 0], nt[:, 0])
                minus(nt[2 * REST:EXT, 2], x32[2 * REST:EXT, 1], nt[2 * REST:EXT, 2])
                minus(ct[:, 2:4], ct32[:], ct[:, 0:2]).then_inc(in_ready, 1)

            def maxima(a, t, which):
                g1, par = STEPS * a + t - 1, (t - 1) % 2
                for i in which:
                    dve.wait_ge(score_ready, NS * g1 + i + 1)
                    j, qt = i // QT, i % QT
                    for s, keys in enumerate((slice(0, TEXT), slice(TEXT, SK))):
                        last = nc.vector.tensor_reduce(negmax[:, par, j, s, qt:qt + 1], pscore[:, i % 2, keys],
                                                       AX.X, ALU.max, negate=True)
                    last.then_inc(max_done, 1)

            def step(a, t):
                g = STEPS * a + t
                if runs(a, t, 1):
                    maxima(a, t, range(0, 4))
                if runs(a, t, 5) and (t - 5) % GROUPS == GROUPS - 1:
                    m = 2 * a + (t - 5) // GROUPS
                    nc.vector.tensor_tensor(xs[:, m], xs[:, m], bo_rows[:], ALU.add).then_inc(biased, 1)
                    dve.wait_ge(biased, m + 1)
                    dve.wait_ge(y_ready, m + 1)
                    nc.vector.tensor_tensor(xs[:, m], xs[:, m], pd[:, 0:QT * C].rearrange("p (q c) -> p q c", q=QT),
                                            ALU.add).then_inc(y_taken, 1)
                if runs(a, t, 1):
                    maxima(a, t, range(4, NS))
                if runs(a, t, 0):
                    par = t % 2
                    fuse = nc.vector.scalar_tensor_tensor
                    dve.wait_ge(a_rounded, g + 1)
                    fuse(out=q4[:], in0=pa[:, 0:SQ], scalar=q_lo, in1=q_signed[:].bitcast(FP32),
                         op0=ALU.mult, op1=ALU.add)
                    fuse(out=k4[:, par, 0:TEXT], in0=pa[:, SQ:SQ + TEXT], scalar=k_lo,
                         in1=k_signed[:, 0:TEXT].bitcast(FP32), op0=ALU.mult, op1=ALU.add).then_inc(q4_done, 1)
                    dve.wait_ge(b_rounded, g + 1)
                    fuse(out=k4[:, par, TEXT:SK], in0=pb[:, TEXT:SK], scalar=k_lo,
                         in1=k_signed[:, TEXT:SK].bitcast(FP32), op0=ALU.mult, op1=ALU.add).then_inc(k4_ready, 1)
                if runs(a, t, 4):
                    g4, par, u4 = g - 4, t % 2, (t - 4) % GROUPS
                    wait(dve, ot_ready, g4)
                    dve.wait_ge(den_ready, g4 + 1)
                    nc.vector.reciprocal(recip[:], pd[:, 0:SQ]).then_inc(recip_done, 1)
                    dve.wait_ge(recip_done, g4 + 1)
                    nc.vector.tensor_tensor(ot[:, u4, :], sums[:, par, :], recip[:], ALU.mult).then_inc(ot_ready, 1)
                if next_batch(a, t) is not None:
                    lo_inputs(next_batch(a, t))

            nc.vector.memset(ones_b[:], 1.0)
            dve.wait_ge(small_in, 80)
            nc.vector.tensor_copy(part[:], part32[:]).then_inc(consts_set, 1)
            dve.wait_ge(v_cleared, 1)
            for vb in range(2):
                nc.vector.memset(v[:, vb, 1:KT, :, 3 * D0:4 * D0], 1.0)
                for s in range(2):
                    cols = slice((2 + s) * D0, (3 + s) * D0)
                    last = nc.vector.tensor_scalar(v[:, vb, 0, :, cols], v[:, vb, 0, :, cols],
                                                   marks[:, 8 + s:9 + s], None, ALU.add)
            last.then_inc(v_marked, 1)
            lo_inputs(0)
            low_w(dve)
            turns(dve, step, 6)

        @block.gpsimd
        def _(pool):
            def step(a, t):
                if runs(a, t, 1):
                    g1, par = STEPS * a + t - 1, (t - 1) % 2
                    wait(pool, exp_done, NB * (g1 - 1))
                    for j in range(GROUP):
                        pool.wait_ge(max_done, NS * g1 + QT * (j + 1))
                        nc.gpsimd.tensor_tensor(diag[:, par, j].rearrange("p s (q c) -> p (s q) c", q=QT),
                                                ident.unsqueeze(1).broadcast_to([P, 2 * QT, P]),
                                                negmax[:, par, j].rearrange("p s q -> p (s q)").unsqueeze(2)
                                                .broadcast_to([P, 2 * QT, P]), ALU.mult).then_inc(diag_ready, 1)

            nc.gpsimd.memset(v[:], 0.0).then_inc(v_cleared, 1)
            turns(pool, step, 6)


def feed_forward_layer(nc, tag, xs, ident, dram, out):
    FT = FF // P

    with ExitStack() as ctx:
        sb = lambda name, shape, dt: ctx.enter_context(nc.sbuf_tensor(f"{tag}_{name}", shape, dt))
        ps = lambda name, shape: ctx.enter_context(nc.psum_tensor(f"{tag}_{name}", shape, FP32))
        sem = lambda name: ctx.enter_context(nc.semaphore(f"{tag}_{name}"))

        w1 = sb("w1", [P, 3, 2 * FF], FP32R)
        w2 = sb("w2", [P, FT, C], FP32)
        b1 = sb("b1", [P, 2 * FT], FP32)
        b2_rows = sb("b2_rows", [P, QT, C], FP32)
        gains = sb("gains", [P, 4], FP32)
        staging = sb("staging", [P, 2, 2 * FF], FP32)
        nt = sb("nt", [P, 3, SQ], FP32R)
        gate = sb("gate", [P, FT, SQ], FP32)
        hidden = sb("hidden", [P, FT, SQ], FP32)
        ph = ps("ph", [P, FT, 512])
        pt, py = ps("pt", [P, 512]), ps("py", [P, 512])

        loaded = [sem("loaded0"), sem("loaded1")]
        rounded, w_done, small_in = sem("rounded"), sem("w_done"), sem("small_in")
        h_ready, gelu_done, hidden_ready = sem("h_ready"), sem("gelu_done"), sem("hidden_ready")
        y_ready, y_taken, stored = sem("y_ready"), sem("y_taken"), sem("stored")

        ln = LayerNorm(nc, ctx, f"{tag}_ln", xs, ident, nt, gains, b2_rows[:], pt)
        pieces = n_weight_pieces(dram["w1"], dram["w1_ext"], w1)
        load_w, high_w, low_w = split_weights(nc, (loaded, rounded, w_done), staging, pieces)
        block = ctx.enter_context(nc.Block())

        @block.sync
        def _(sp):
            for place, name in ((gains, "gains"), (b2_rows, "b2_rows"), (b1, "b1"), (w2, "w2")):
                sp.dma_start(place[:], dram[name]).then_inc(small_in, 16)
            load_w(sp)
            with sp.Fori(0, B) as b:
                sp.wait_ge(y_taken, b + 1)
                sp.dma_start(out[b], xs[:, b]).then_inc(stored, 16)
            sp.wait_ge(stored, 16 * B)

        @block.tensor
        def _(pe):
            mm = nc.tensor.matmul

            def batch(b):
                pe.wait_ge(ln.n_ready, b + 1)
                for i in range(FT):
                    wait(pe, hidden_ready, FT * (b - 1) + i + 1)
                    for s in range(2):
                        cols = slice((s * FT + i) * P, (s * FT + i + 1) * P)
                        for k, (ws, xs_, rows) in enumerate(N_TERMS):
                            last = mm(ph[:, i, s * SQ:(s + 1) * SQ], w1[0:rows, ws, cols], nt[0:rows, xs_, :],
                                      start=k == 0, stop=k == len(N_TERMS) - 1)
                    last.then_inc(h_ready, 1)
                if not is_last(b):
                    ln.pe_transpose(pe, b + 1)
                wait(pe, y_taken, b)
                for qt in range(QT):
                    for i in range(FT):
                        pe.wait_ge(hidden_ready, FT * b + i + 1)
                        last = mm(py[:, qt * C:(qt + 1) * C], hidden[:, i, qt * P:(qt + 1) * P], w2[:, i, :],
                                  start=i == 0, stop=i == FT - 1)
                last.then_inc(y_ready, 1)

            pe.wait_ge(small_in, 64)
            ln.pe_transpose(pe, 0)
            pe.wait_ge(w_done, len(pieces))
            over_batches(pe, batch)

        @block.scalar
        def _(act):
            def batch(b):
                for i in range(FT):
                    act.wait_ge(h_ready, FT * b + i + 1)
                    nc.scalar.activation(gate[:, i, :], ph[:, i, SQ:2 * SQ], ACT.Gelu,
                                         bias=b1[:, FT + i:FT + i + 1]).then_inc(gelu_done, 1)
                if not is_last(b):
                    ln.act_hi(act, b + 1)

            high_w(act)
            act.wait_ge(small_in, 64)
            ln.act_hi(act, 0)
            over_batches(act, batch)

        @block.vector
        def _(dve):
            def batch(b):
                if not is_last(b):
                    ln.dve_stats(dve, b + 1)
                    ln.dve_xhat(dve, b + 1)
                for i in range(FT):
                    dve.wait_ge(gelu_done, FT * b + i + 1)
                    nc.vector.scalar_tensor_tensor(out=hidden[:, i, :], in0=ph[:, i, 0:SQ], scalar=b1[:, i:i + 1],
                                                   in1=gate[:, i, :], op0=ALU.add,
                                                   op1=ALU.mult).then_inc(hidden_ready, 1)
                if not is_last(b):
                    ln.dve_n32(dve, b + 1)
                    ln.dve_lo(dve, b + 1)
                dve.wait_ge(y_ready, b + 1)
                dve.wait_ge(ln.biased, b + 1)
                nc.vector.tensor_tensor(xs[:, b], xs[:, b], py[:, 0:QT * C].rearrange("p (q c) -> p q c", q=QT),
                                        ALU.add).then_inc(y_taken, 1)

            dve.wait_ge(small_in, 64)
            ln.dve_stats(dve, 0)
            ln.dve_xhat(dve, 0)
            ln.dve_n32(dve, 0)
            low_w(dve)
            ln.dve_lo(dve, 0)
            over_batches(dve, batch)

        @block.gpsimd
        def _(pool):
            ln.pool_setup(pool)
            ln.pool_rstd(pool, 0)
            with pool.Fori(1, B) as b:
                ln.pool_rstd(pool, b)


def build(nc, t, out):
    with ExitStack() as ctx:
        xs = ctx.enter_context(nc.sbuf_tensor("xs", [P, B, QT, C], FP32))
        ident = ctx.enter_context(nc.sbuf_tensor("identity", [P, P], FP32))
        inputs_in = ctx.enter_context(nc.semaphore("inputs_in"))
        with nc.Block() as block:
            @block.sync
            def _(sp):
                sp.dma_start(ident[:], t["ident"]).then_inc(inputs_in, 16)
                with sp.Fori(0, B) as b:
                    sp.dma_start(xs[:, b], t["x"][b]).then_inc(inputs_in, 16)
                sp.wait_ge(inputs_in, 16 * (B + 1))
        narrow_attention_layer(nc, "l0", xs, ident[:], t["l0"], t["x_t"], t["ctx_t"])
        attention_layer(nc, "a1", xs, ident[:], t["a1"], None)
        attention_layer(nc, "a2", xs, ident[:], t["a2"], t["ctx_t"])
        feed_forward_layer(nc, "ff", xs, ident[:], t["ff"], out)


def laid_out(inputs):
    x, ctx = inputs["x"], inputs["ctx_2048"]
    halves = lambda w: w.reshape(2, P, w.shape[-1])
    main = lambda w: w[:P]
    ext = lambda w: np.concatenate([w[P:]] * 3)
    rows = lambda bias: np.broadcast_to(bias, (P, QT, C))
    by_tile = lambda w: w.reshape(-1, P, w.shape[-1]).transpose(1, 0, 2)

    arrays = {"ident": np.eye(P, dtype=np.float32),
              "x": x.reshape(B, QT, P, C).transpose(0, 2, 1, 3),
              "ctx_t": ctx.transpose(0, 2, 1).reshape(B, 2, P, SK).transpose(0, 2, 1, 3)}
    x_t = x.transpose(0, 2, 1)
    both = np.zeros((B, P, 2, SQ), np.float32)
    both[:, :, 0] = x_t[:, :P]
    both[:, :EXT, 1] = np.concatenate([x_t[:, P:]] * 3, axis=1)
    arrays["x_t"] = both

    repeat = lambda w: np.broadcast_to(w.reshape(-1, HEADS, 1, D0), (w.shape[0], HEADS, 4, D0)).reshape(w.shape[0], -1)
    w0 = {k: inputs[f"L0_xattn_{k}"].T for k in ("Wq", "Wk", "Wv", "Wk_ip", "Wv_ip", "Wo")}
    wq = repeat(w0["Wq"])
    marks = np.zeros((P, 12), np.float32)
    r = np.arange(P) % ROWS // D0
    marks[:, 0], marks[:, 1] = r % 2, 1 - 2 * (r % 2)
    marks[:, 2], marks[:, 3] = r // 2, 1 - 2 * (r // 2)
    for j in range(GROUP):
        marks[j * ROWS:(j + 1) * ROWS, 4 + j] = 1
    marks[:TEXT, 8] = 1
    marks[TEXT:, 9] = 1
    part = np.zeros((P, 2, P), np.float32)
    part[:, 0, :TEXT] = 1
    part[:, 1, TEXT:] = 1
    pick = np.zeros((P, P), np.float32)
    m = np.arange(P)
    pick[np.where(m % ROWS < 2 * D0, m + 2 * D0, m), m] = 1
    wo = np.zeros((GROUPS, GROUP, 4, D0, C), np.float32)
    wo[:, :, 0] = wo[:, :, 1] = w0["Wo"].reshape(GROUPS, GROUP, D0, C)
    layers = {"l0": {"wq": main(wq), "wq_ext": ext(wq), "wk": halves(repeat(w0["Wk"])),
                     "wk_ip": halves(repeat(w0["Wk_ip"])),
                     "wv": halves(np.concatenate([w0["Wv"], w0["Wv_ip"]], axis=1)),
                     "wo": wo.reshape(GROUPS, P, C).transpose(1, 0, 2), "bo_rows": rows(inputs["L0_xattn_bo"]),
                     "marks": marks, "part": part, "pick": pick}}

    def gains(n):
        g, b = inputs[f"L1_xattn_{n}_g"], inputs[f"L1_xattn_{n}_b"]
        out = np.zeros((P, 4), np.float32)
        out[:, 0], out[:, 1] = g[:P], b[:P]
        out[:EXT, 2], out[:EXT, 3] = np.concatenate([g[P:]] * 3), np.concatenate([b[P:]] * 3)
        return out

    for a, n in (("a1", "ln1"), ("a2", "ln2")):
        w = {k: inputs[f"L1_xattn_{a}_{k}"] for k in ("wq", "wk", "wv", "wo", "bo")}
        layers[a] = {"wq": main(w["wq"]), "wq_ext": ext(w["wq"]), "wo": by_tile(w["wo"]),
                     "bo_rows": rows(w["bo"]), "gains": gains(n)}
        for k in ("wk", "wv"):
            if a == "a1":
                layers[a] |= {k: main(w[k]), k + "_ext": ext(w[k])}
            else:
                layers[a][k] = halves(w[k])
    w1 = inputs["L1_xattn_ff_w1"]
    layers["ff"] = {"w1": main(w1), "w1_ext": ext(w1), "w2": by_tile(inputs["L1_xattn_ff_w2"]),
                    "b1": inputs["L1_xattn_ff_b1"].reshape(-1, P).T, "b2_rows": rows(inputs["L1_xattn_ff_b2"]),
                    "gains": gains("ln3")}
    for layer, named in layers.items():
        arrays |= {f"{layer}.{name}": a for name, a in named.items()}
    return arrays


def kernel(**inputs):
    from concourse import bacc
    from concourse.bass_utils import run_bass_kernel_spmd

    inputs = {k: np.asarray(v) for k, v in inputs.items()}
    arrays = {f"in_{k.replace('.', '_')}": np.ascontiguousarray(a) for k, a in laid_out(inputs).items()}
    nc = bacc.Bacc("TRN2", target_bir_lowering=False, num_devices=1)
    t = {}
    for key in laid_out(inputs):
        name = f"in_{key.replace('.', '_')}"
        a = arrays[name]
        ap = nc.dram_tensor(name, a.shape, mybir.dt.from_np(a.dtype), kind="ExternalInput").ap()
        if "." in key:
            layer, part = key.split(".")
            t.setdefault(layer, {})[part] = ap
        else:
            t[key] = ap
    out = nc.dram_tensor("out", (B, P, QT, C), FP32, kind="ExternalOutput").ap()
    build(nc, t, out)
    r = run_bass_kernel_spmd(nc, [arrays], core_ids=[0])
    return r.results[0]["out"].transpose(0, 2, 1, 3).reshape(B, SQ, C)
```

```python
import numpy as np
import concourse.bass as bass
from concourse import mybir
from contextlib import ExitStack

FP32 = mybir.dt.float32
FP32R = mybir.dt.float32r
BF16 = mybir.dt.bfloat16
ALU = mybir.AluOpType
ACT = mybir.ActivationFunctionType
AX = mybir.AxisListType

B, SQ, C = 8, 256, 160
SK, CC = 512, 256
TEXT = 77
HEADS = 20
D0 = C // HEADS
D1 = 64
INNER = HEADS * D1
FF = 4 * C
P = 128
QT = SQ // P
REST = C - P
EXT = 3 * REST
PAIRS = HEADS // 2
HALF = PAIRS // 2
DVE_PIECES, POOL_PIECES = (1, 2, 3, 5), (0, 4)
BUFS = 5
EPS = 1e-5

N_TERMS = [(0, 0, P), (1, 0, P), (0, 1, P), (2, 2, EXT)]
CTX_TERMS = [(0, 0, P), (1, 1, P), (2, 0, P), (3, 1, P), (0, 2, P), (1, 3, P)]


def wait(eng, sem, value):
    if isinstance(value, int) and value <= 0:
        return
    eng.wait_ge(sem, value)


def over_batches(eng, body):
    body(0)
    with eng.Fori(1, B - 1) as b:
        body(b)
    body(B - 1)


def is_last(b):
    return isinstance(b, int) and b == B - 1


class Weights:

    def __init__(self, nc, ctx, tag, raw, width, n_pieces, one_by_one):
        sem = lambda name: ctx.enter_context(nc.semaphore(f"{tag}_{name}"))
        self.nc, self.raw, self.width = nc, raw, width
        self.one_by_one, self.n_pieces = one_by_one, n_pieces
        self.loaded = [sem(f"loaded{k}") for k in range(n_pieces if one_by_one else 1)]
        self.rounded = sem("rounded")
        self.done = sem("w_done")

    def place(self, k, rows, cols):
        r0, r1 = rows
        return self.raw[r0:r1, k * self.width:k * self.width + cols]

    def load(self, sp, sources):
        for k, (src, rows) in enumerate(sources):
            arrived = self.loaded[k if self.one_by_one else 0]
            sp.dma_start(self.place(k, (0, rows), src.shape[1]), src).then_inc(arrived, 16)

    def high(self, act, pieces):
        for k, (src, rows, hi, _, _) in enumerate(pieces):
            if self.one_by_one:
                act.wait_ge(self.loaded[k], 16)
            elif k == 0:
                act.wait_ge(self.loaded[0], 16 * self.n_pieces)
            self.nc.scalar.activation(hi, self.place(k, (0, rows), src.shape[1]), ACT.Copy).then_inc(self.rounded, 1)

    def low(self, eng, tensor_tensor, pieces, which):
        for k in which:
            src, rows, hi, lo, lo_rows = pieces[k]
            eng.wait_ge(self.rounded, k + 1)
            minus = lo if lo_rows != (0, rows) else hi
            tensor_tensor(lo, self.place(k, lo_rows, src.shape[1]), minus.bitcast(FP32),
                          ALU.subtract).then_inc(self.done, 1)


def weight_sources(dram, ext_of, halves_of):
    out = []
    for name in ext_of:
        out += [(dram[name], P), (dram[name + "_ext"], EXT)]
    for name in halves_of:
        out += [(dram[name][half], P) for half in range(2)]
    return out


def n_weight_pieces(src_main, src_ext, slots):
    return [(src_main, P, slots[:, 0, :], slots[:, 1, :], (0, P)),
            (src_ext, EXT, slots[0:EXT, 2, :], slots[REST:2 * REST, 2, :], (REST, 2 * REST))]


class LayerNorm:

    def __init__(self, nc, ctx, tag, xs, ident, n_terms, gains, bias_rows, psum):
        sb = lambda name, shape, dt: ctx.enter_context(nc.sbuf_tensor(f"{tag}_{name}", shape, dt))
        sem = lambda name: ctx.enter_context(nc.semaphore(f"{tag}_{name}"))
        self.nc, self.xs, self.ident, self.nt, self.gains, self.rows, self.psum = (
            nc, xs, ident, n_terms, gains, bias_rows, psum)
        self.stats = sb("stats", [P, QT, 6], FP32)
        self.mv = sb("mv", [P, QT, 2], FP32)
        self.var = sb("var", [P, QT], FP32)
        self.aggregated = sb("aggregated", [P, 1], FP32)
        self.rstd = sb("rstd", [P, QT], FP32)
        self.half = sb("half", [P, QT], FP32)
        self.xhat = sb("xhat", [P, QT, P + EXT], FP32)
        self.n32 = [sb("n32", [P, SQ], FP32), sb("n32_ext", [EXT, SQ], FP32)]
        self.half_set = sem("half_set")
        self.stats_chain = sem("stats_chain")
        self.var_ready = sem("var_ready")
        self.rstd_ready = sem("rstd_ready")
        self.xhat_ready = sem("xhat_ready")
        self.biased = sem("biased")
        self.t_ready = sem("t_ready")
        self.n32_ready = sem("n32_ready")
        self.n_hi = sem("n_hi")
        self.n_ready = sem("n_ready")

    def pool_setup(self, pool):
        self.nc.gpsimd.memset(self.half[:], -0.5).then_inc(self.half_set, 1)
        pool.wait_ge(self.half_set, 1)

    def dve_stats(self, dve, m):
        nc = self.nc
        for qt in range(QT):
            last = nc.vector.bn_stats(self.stats[:, qt], self.xs[:, m, qt])
        last.then_inc(self.stats_chain, 1)
        wait(dve, self.stats_chain, 2 * m + 1)
        nc.vector.memset(self.aggregated[:], 0.0)
        for qt in range(QT):
            last = nc.vector.bn_aggr(self.mv[:, qt], self.stats[:, qt])
        last.then_inc(self.stats_chain, 1)
        wait(dve, self.stats_chain, 2 * m + 2)
        nc.vector.tensor_scalar(self.var[:], self.mv[:, :, 1], EPS, None, ALU.add).then_inc(self.var_ready, 1)

    def pool_rstd(self, pool, m):
        pool.wait_ge(self.var_ready, m + 1)
        self.nc.gpsimd.tensor_tensor(self.rstd[:], self.var[:], self.half[:], ALU.pow).then_inc(self.rstd_ready, 1)

    def dve_xhat(self, dve, m):
        nc = self.nc
        dve.wait_ge(self.rstd_ready, m + 1)
        for qt in range(QT):
            scalars = (self.mv[:, qt, 0:1], self.rstd[:, qt:qt + 1])
            nc.vector.tensor_scalar(self.xhat[:, qt, 0:C], self.xs[:, m, qt], *scalars, ALU.subtract, ALU.mult)
            for r in range(1, 3):
                last = nc.vector.tensor_scalar(self.xhat[:, qt, P + r * REST:P + (r + 1) * REST],
                                               self.xs[:, m, qt, P:C], *scalars, ALU.subtract, ALU.mult)
        last.then_inc(self.xhat_ready, 1)
        dve.wait_ge(self.xhat_ready, m + 1)
        nc.vector.tensor_tensor(self.xs[:, m], self.xs[:, m], self.rows, ALU.add).then_inc(self.biased, 1)

    def pe_transpose(self, pe, m):
        nc = self.nc
        pe.wait_ge(self.xhat_ready, m + 1)
        for qt in range(QT):
            nc.tensor.transpose(self.psum[:, qt * P:(qt + 1) * P], self.xhat[:, qt, 0:P], self.ident)
        for qt in range(QT):
            last = nc.tensor.transpose(self.psum[0:EXT, SQ + qt * P:SQ + (qt + 1) * P],
                                       self.xhat[:, qt, P:P + EXT], self.ident)
        last.then_inc(self.t_ready, 1)

    def dve_n32(self, dve, m):
        nc = self.nc
        dve.wait_ge(self.t_ready, m + 1)
        g, gains = self.gains, nc.vector.tensor_scalar
        gains(self.n32[0][:], self.psum[:, 0:SQ], g[:, 0:1], g[:, 1:2], ALU.mult, ALU.add)
        gains(self.n32[1][:], self.psum[0:EXT, SQ:2 * SQ], g[0:EXT, 2:3], g[0:EXT, 3:4],
              ALU.mult, ALU.add).then_inc(self.n32_ready, 1)

    def act_hi(self, act, m):
        nc = self.nc
        act.wait_ge(self.n32_ready, m + 1)
        nc.scalar.activation(self.nt[:, 0], self.n32[0][:], ACT.Copy)
        nc.scalar.activation(self.nt[0:EXT, 2], self.n32[1][:], ACT.Copy).then_inc(self.n_hi, 1)

    def dve_lo(self, dve, m):
        nc = self.nc
        dve.wait_ge(self.n_hi, m + 1)
        nc.vector.tensor_tensor(self.nt[:, 1], self.n32[0][:], self.nt[:, 0].bitcast(FP32), ALU.subtract)
        lo = self.nt[2 * REST:EXT, 2]
        nc.vector.tensor_tensor(lo, self.n32[1][2 * REST:EXT], lo.bitcast(FP32),
                                ALU.subtract).then_inc(self.n_ready, 1)


def attention_layer(nc, tag, xs, ident, dram, ctx_t, raw, weights, load_next):
    cross = ctx_t is not None
    NK = SK if cross else SQ
    KT = NK // P
    KB = KT // 2
    NB = 2 * KB
    NS = 2 * QT if cross else 2
    KSLOTS = 4 if cross else 3
    K_TERMS = CTX_TERMS if cross else N_TERMS
    SCALE = float(D1) ** -0.5
    total = PAIRS * B

    with ExitStack() as ctx:
        sb = lambda name, shape, dt: ctx.enter_context(nc.sbuf_tensor(f"{tag}_{name}", shape, dt))
        ps = lambda name, shape: ctx.enter_context(nc.psum_tensor(f"{tag}_{name}", shape, FP32))
        sem = lambda name: ctx.enter_context(nc.semaphore(f"{tag}_{name}"))

        wq = sb("wq", [P, 3, INNER], FP32R)
        wk = sb("wk", [P, KSLOTS, INNER], FP32R)
        wv = sb("wv", [P, KSLOTS, INNER], FP32R)
        wo = sb("wo", [P, PAIRS, C], FP32)
        gains = sb("gains", [P, 4], FP32)
        bo_rows = sb("bo_rows", [P, QT, C], FP32)
        ones = sb("ones", [P, D1], FP32)
        nt = sb("nt", [P, 3, SQ], FP32R)
        q1 = sb("q1", [P, BUFS, 2, SQ], FP32R)
        k1 = sb("k1", [P, BUFS, 2, NK], FP32R)
        q2 = sb("q2", [P, BUFS, 2, SQ], FP32R)
        k2 = sb("k2", [P, BUFS, 2, NK], FP32R)
        v = sb("v", [P, KT, INNER], FP32)
        negmax = sb("negmax", [P, 2, QT, 2], FP32)
        recip = sb("recip", [P, SQ], FP32)
        if cross:
            cut = lambda start, size: raw[:, start:start + size]
            n_probs, n_ot, n_sum = 4 * KT * SQ, HALF * SQ, 4 * SQ
            probs = cut(0, n_probs).rearrange("p (b h k q) -> p b h k q", b=2, h=2, k=KT)
            ot = cut(n_probs, n_ot).rearrange("p (s q) -> p s q", s=HALF)
            key_sum = cut(n_probs + n_ot, n_sum).rearrange("p (b h q) -> p b h q", b=2, h=2)
            half_sum = cut(n_probs + n_ot + n_sum, n_sum).rearrange("p (h k q) -> p h k q", h=2, k=2)
        else:
            probs = sb("probs", [P, 2, 2, KT, SQ], FP32)[:]
            key_sum = sb("key_sum", [P, 2, 2, SQ], FP32)[:]
            ot = sb("ot", [P, HALF, SQ], FP32)[:]
        if cross:
            ct32 = sb("ct32", [P, 2, NK], FP32)
            ct = sb("ct", [P, 4, NK], FP32R)
        pa, pb, pv, py = (ps(name, [P, 512]) for name in ("pa", "pb", "pv", "py"))
        pscore = ps("pscore", [P, 2, 512])
        pst = ps("pst", [P, 2, 512])

        small_in, wo_in = sem("small_in"), sem("wo_in")
        q2_zeroed, k2_zeroed, ones_set = sem("q2_zeroed"), sem("k2_zeroed"), sem("ones_set")
        ctx_in, c_hi, c_ready = sem("ctx_in"), sem("c_hi"), sem("c_ready")
        q_ready, q_hi, q_copied, q_split = (sem(f"q_{s}") for s in ("ready", "hi", "copied", "split"))
        k_ready, k_hi, k_copied, k_split = (sem(f"k_{s}") for s in ("ready", "hi", "copied", "split"))
        v_ready, v_copied = sem("v_ready"), sem("v_copied")
        score_ready, max_done = sem("score_ready"), sem("max_done")
        max_turned, max_placed, rows_set = sem("max_turned"), sem("max_placed"), sem("rows_set")
        st_ready, exp_done = sem("st_ready"), sem("exp_done")
        half_done, sum_ready = sem("half_done"), sem("sum_ready")
        pv_done, recip_done, ot_ready = sem("pv_done"), sem("recip_done"), sem("ot_ready")
        y_ready, y_taken = sem("y_ready"), sem("y_taken")

        ln = LayerNorm(nc, ctx, f"{tag}_ln", xs, ident, nt, gains, bo_rows[:], py)
        pieces = n_weight_pieces(dram["wq"], dram["wq_ext"], wq)
        if cross:
            for w, src in ((wk, dram["wk"]), (wv, dram["wv"])):
                for half in range(2):
                    pieces.append((src[half], P, w[:, half, :], w[:, 2 + half, :], (0, P)))
        else:
            pieces += n_weight_pieces(dram["wk"], dram["wk_ext"], wk)
            pieces += n_weight_pieces(dram["wv"], dram["wv_ext"], wv)

        def runs(b, t, lag):
            return not isinstance(b, int) or 0 <= PAIRS * b + t - lag < total

        def tail(body):
            for t in range(PAIRS, PAIRS + 5):
                body(B - 1, t)

        def has_output(b, t):
            return t in (HALF + 4, PAIRS + 4) or (t == 4 and runs(b, t, PAIRS))

        def outputs(b, t):
            return 2 * b + {4: 0, HALF + 4: 1, PAIRS + 4: 2}[t]

        v_banks = [(pb, k_split, 2), (pa, q_split, 1)] if cross else [(pa, q_split, 1)]
        own = [slice(h * D1, (h + 1) * D1) for h in range(2)]
        other = [slice((1 - h) * D1, (2 - h) * D1) for h in range(2)]
        extra = [slice((1 - h) * D1, (1 - h) * D1 + 2) for h in range(2)]

        block = ctx.enter_context(nc.Block())

        @block.sync
        def _(sp):
            sp.dma_start(gains[:], dram["gains"]).then_inc(small_in, 16)
            sp.dma_start(bo_rows[:], dram["bo_rows"]).then_inc(small_in, 16)
            if cross:
                sp.dma_start(ct32[:], ctx_t[0]).then_inc(ctx_in, 16)
            sp.dma_start(wo[:], dram["wo"]).then_inc(wo_in, 16)
            if load_next:
                sp.wait_ge(weights.done, len(pieces))
                load_next(sp)
            if cross:
                with sp.Fori(1, B) as b:
                    sp.wait_ge(c_ready, b)
                    sp.dma_start(ct32[:], ctx_t[b]).then_inc(ctx_in, 16)

        @block.tensor
        def _(pe):
            mm = nc.tensor.matmul

            def score(b, t, i):
                g2, buf = PAIRS * b + t - 2, (t - 2) % BUFS
                if i % (NS // 2) == 0:
                    h = i // (NS // 2)
                    wait(pe, q_copied, 2 * g2 + h + 1)
                    wait(pe, k_copied, 2 * g2 + h + 1)
                    wait(pe, k_split, 2 * g2 + h + 1)
                wait(pe, max_done, NS * g2 + i - 1)
                if cross:
                    last = mm(pscore[:, i % 2, :], q1[:, buf, i // QT, (i % QT) * P:(i % QT + 1) * P],
                              k1[:, buf, i // QT, :], start=True, stop=True)
                else:
                    for qt in range(QT):
                        last = mm(pscore[:, i % 2, qt * NK:(qt + 1) * NK], q1[:, buf, i, qt * P:(qt + 1) * P],
                                  k1[:, buf, i, :], start=True, stop=True)
                last.then_inc(score_ready, 1)

            def turned_scores(b, t, n):
                g3, buf, h, kb = PAIRS * b + t - 3, (t - 3) % BUFS, n // KB, n % KB
                if n == 0:
                    wait(pe, max_placed, g3 + 1)
                    if isinstance(b, int) and b == 0 and t < BUFS + 3:
                        pe.wait_ge(q2_zeroed, 2)
                        pe.wait_ge(rows_set, t - 2)
                    wait(pe, q_split, g3 + 1)
                wait(pe, exp_done, NB * g3 + n - 1)
                for j in range(2):
                    out = pst[:, n % 2, j * SQ:(j + 1) * SQ]
                    kt = slice((2 * kb + j) * P, (2 * kb + j + 1) * P)
                    mm(out, k1[:, buf, h, kt], q1[:, buf, h, :], start=True, stop=False)
                    last = mm(out, k2[:, buf, h, kt], q2[:, buf, h, :], start=False, stop=True)
                last.then_inc(st_ready, 1)

            def queries(b, t):
                g = PAIRS * b + t
                if t == 0 and cross:
                    pe.wait_ge(ln.n_ready, b + 1)
                if t % 2 == 1:
                    pe.wait_ge(v_copied, KB * (HALF * b + t // 2 + 1))
                else:
                    wait(pe, q_split, g)
                for i, (ws, xs_, rows) in enumerate(N_TERMS):
                    last = mm(pa[:, 0:SQ], wq[0:rows, ws, t * P:(t + 1) * P], nt[0:rows, xs_, :],
                              start=i == 0, stop=i == len(N_TERMS) - 1)
                last.then_inc(q_ready, 1)

            def keys(b, t, part):
                g = PAIRS * b + t
                if part == 0:
                    if t == 0:
                        pe.wait_ge(c_ready if cross else ln.n_ready, b + 1)
                    wait(pe, k_split, 2 * g)
                    if cross and t % 2 == 1:
                        pe.wait_ge(v_copied, KB * (HALF * b + t // 2) + 1)
                half = len(K_TERMS) // 2
                for i in range(part * half, (part + 1) * half):
                    ws, xs_, rows = K_TERMS[i]
                    last = mm(pb[:, 0:NK], wk[0:rows, ws, t * P:(t + 1) * P], (ct if cross else nt)[0:rows, xs_, :],
                              start=i == 0, stop=i == len(K_TERMS) - 1)
                if part == 1:
                    last.then_inc(k_ready, 1)

            def values(b, t):
                g = PAIRS * b + t
                acts = ct if cross else nt
                for kb in range(KB):
                    bank, split, heads = v_banks[kb]
                    wait(pe, split, heads * (g + 1))
                    for j in range(2):
                        kt = 2 * kb + j
                        for i, (ws, xs_, rows) in enumerate(K_TERMS):
                            last = mm(bank[:, j * 256:(j + 1) * 256], acts[0:rows, xs_, kt * P:(kt + 1) * P],
                                      wv[0:rows, ws, t * P:t * P + 256], start=i == 0, stop=i == len(K_TERMS) - 1)
                    last.then_inc(v_ready, 1)

            def weighted_sums(b, t):
                g4, par, p = PAIRS * b + t - 4, (t - 4) % 2, (t - 4) % PAIRS
                wait(pe, ot_ready, g4)
                wait(pe, exp_done, NB * (g4 + 1))
                for kt in range(KT):
                    for h in range(2):
                        c0 = p * P + h * D1
                        mm(pv[own[h], 0:SQ], v[:, kt, c0:c0 + D1], probs[:, par, h, kt, :],
                           start=kt == 0, stop=kt == KT - 1)
                wait(pe, sum_ready, 2 * (g4 + 1))
                for h in range(2):
                    last = mm(pv[own[h], SQ:2 * SQ], ones[:], key_sum[:, par, h, :], start=True, stop=True)
                last.then_inc(pv_done, 1)

            def output(b, t):
                g = PAIRS * b + t
                wait(pe, ot_ready, g - 4)
                wait(pe, max_placed, total if t >= PAIRS else g - 2)
                first = 0 if t == HALF + 4 else HALF
                for qt in range(QT):
                    for p in range(HALF):
                        last = mm(py[:, qt * C:(qt + 1) * C], ot[:, p, qt * P:(qt + 1) * P], wo[:, first + p, :],
                                  start=p == 0, stop=p == HALF - 1)
                last.then_inc(y_ready, 1)

            def step(b, t):
                g = PAIRS * b + t
                for n in range(NB):
                    if runs(b, t, 2):
                        score(b, t, n)
                    if runs(b, t, 0):
                        if n < NB // 2:
                            for part in range(2) if NB == 2 else (n,):
                                keys(b, t, part)
                        if n == NB // 2:
                            queries(b, t)
                    if runs(b, t, 3):
                        turned_scores(b, t, n)
                if has_output(b, t):
                    output(b, t)
                if runs(b, t, 4):
                    weighted_sums(b, t)
                if runs(b, t, 2):
                    wait(pe, max_done, NS * (g - 1))
                    if has_output(b, t):
                        pe.wait_ge(y_taken, outputs(b, t))
                    if runs(b, t, 0) and t == 7 and not is_last(b):
                        pe.wait_ge(ln.n32_ready, b + 2)
                    for qt in range(QT):
                        last = nc.tensor.transpose(py[0:2, qt * P:(qt + 1) * P], negmax[:, t % 2, qt, :], ident)
                    last.then_inc(max_turned, 1)
                if runs(b, t, 0) and t == 6 and not is_last(b):
                    pe.wait_ge(max_placed, g - 1)
                    ln.pe_transpose(pe, b + 1)
                if runs(b, t, 0) and t % 2 == 0:
                    values(b, t)

            ln.pe_transpose(pe, 0)
            pe.wait_ge(weights.done, len(pieces))
            pe.wait_ge(ones_set, 1)
            pe.wait_ge(wo_in, 16)
            over_batches(pe, lambda b: [step(b, t) for t in range(PAIRS)])
            tail(step)

        @block.scalar
        def _(act):
            def hi_ctx(m):
                act.wait_ge(ctx_in, 16 * (m + 1))
                nc.scalar.activation(ct[:, 0:2], ct32[:], ACT.Copy).then_inc(c_hi, 1)

            def exp(b, t, n):
                g3, par, h, kb = PAIRS * b + t - 3, (t - 3) % 2, n // KB, n % KB
                if n == 0:
                    wait(act, pv_done, g3 - 1)
                act.wait_ge(st_ready, NB * g3 + n + 1)
                nc.scalar.activation(probs[:, par, h, 2 * kb:2 * kb + 2, :],
                                     pst[:, n % 2, :].rearrange("p (k q) -> p k q", k=2),
                                     ACT.Exp, scale=SCALE).then_inc(exp_done, 1)

            def step(b, t):
                g, buf = PAIRS * b + t, t % BUFS
                if isinstance(b, int) and b == 0 and 1 <= t <= BUFS:
                    act.wait_ge(k2_zeroed, 2)
                    for h in range(2):
                        last = nc.scalar.activation(k2[extra[h], t - 1, h, :],
                                                    ident[0:2, h:h + 1].broadcast_to([2, NK]), ACT.Copy)
                    last.then_inc(rows_set, 1)
                k_at = NB // 2 - 1 if cross else -1
                for n in range(-1, NB):
                    if runs(b, t, 3) and n >= 0:
                        exp(b, t, n)
                    if runs(b, t, 0) and n == k_at:
                        act.wait_ge(k_ready, g + 1)
                        for h in range(2):
                            nc.scalar.activation(k2[own[h], buf, h, :], pb[own[h], 0:NK], ACT.Copy).then_inc(k_hi, 1)
                        for h in range(2):
                            act.wait_ge(k_hi, 2 * g + h + 1)
                            nc.scalar.activation(k1[own[h], buf, h, :], k2[own[h], buf, h, :].bitcast(FP32),
                                                 ACT.Copy).then_inc(k_copied, 1)
                if runs(b, t, 0) and t == PAIRS - 1 and cross and not is_last(b):
                    hi_ctx(b + 1)
                if runs(b, t, 0):
                    act.wait_ge(q_ready, g + 1)
                    for h in range(2):
                        nc.scalar.activation(q1[own[h], buf, h, :], pa[own[h], 0:SQ], ACT.Copy).then_inc(q_hi, 1)
                    if t == PAIRS - 1 and not is_last(b):
                        ln.act_hi(act, b + 1)
                if runs(b, t, 2):
                    act.wait_ge(max_turned, g - 1)
                    if isinstance(b, int) and b == 0 and t == 2:
                        act.wait_ge(q2_zeroed, 2)
                    for h in range(2):
                        last = nc.scalar.activation(q2[extra[h], (t - 2) % BUFS, h, :], py[0:2, 0:SQ], ACT.Copy)
                    last.then_inc(max_placed, 1)
                if runs(b, t, 0):
                    for h in range(2):
                        act.wait_ge(q_hi, 2 * g + h + 1)
                        nc.scalar.activation(q1[other[h], buf, h, :], q1[own[h], buf, h, :].bitcast(FP32),
                                             ACT.Copy).then_inc(q_copied, 1)
                if runs(b, t, 0):
                    if t % 2 == 0:
                        for kb in range(KB):
                            act.wait_ge(v_ready, KB * (HALF * b + t // 2) + kb + 1)
                            nc.scalar.activation(v[:, 2 * kb:2 * kb + 2, t * P:t * P + 256],
                                                 v_banks[kb][0][:].rearrange("p (k c) -> p k c", k=2),
                                                 ACT.Copy).then_inc(v_copied, 1)

            weights.high(act, pieces)
            ln.act_hi(act, 0)
            if cross:
                hi_ctx(0)
            over_batches(act, lambda b: [step(b, t) for t in range(PAIRS)])
            tail(step)

        @block.vector
        def _(dve):
            def lo_ctx(m):
                dve.wait_ge(c_hi, m + 1)
                nc.vector.tensor_tensor(ct[:, 2:4], ct32[:], ct[:, 0:2].bitcast(FP32),
                                        ALU.subtract).then_inc(c_ready, 1)

            def invert(half, g5):
                part = slice(half * SQ // 2, (half + 1) * SQ // 2)
                nc.vector.reciprocal(recip[:, part], pv[:, SQ + part.start:SQ + part.stop]).then_inc(recip_done, 1)

            def normalise(b, t):
                dve.wait_ge(recip_done, 2 * (PAIRS * b + t - 4))
                nc.vector.tensor_tensor(ot[:, (t - 5) % HALF, :], pv[:, 0:SQ], recip[:], ALU.mult).then_inc(ot_ready, 1)

            def key_low(b, t, h):
                if runs(b, t, 0):
                    dve.wait_ge(k_hi, 2 * (PAIRS * b + t) + h + 1)
                    nc.vector.tensor_tensor(k1[other[h], t % BUFS, h, :], pb[own[h], 0:NK],
                                            k2[own[h], t % BUFS, h, :].bitcast(FP32), ALU.subtract).then_inc(k_split, 1)

            def step(b, t):
                g, buf = PAIRS * b + t, t % BUFS
                if runs(b, t, 5):
                    g5, slot = g - 5, (t - 5) % HALF
                    if slot == 0:
                        wait(dve, y_ready, 2 * b + {0: -1, HALF: 0, PAIRS: 1}[t])
                    wait(dve, ot_ready, g5)
                    dve.wait_ge(pv_done, g5 + 1)
                    invert(0, g5)
                    if not cross:
                        invert(1, g5)
                        normalise(b, t)
                if t == 0 and cross and runs(b, t, 2):
                    ln.dve_lo(dve, b)
                if runs(b, t, 2):
                    g2, par = g - 2, t % 2
                    for i in range(NS):
                        dve.wait_ge(score_ready, NS * g2 + i + 1)
                        if cross:
                            h, qt = i // QT, i % QT
                            out, src = negmax[:, par, qt, h:h + 1], pscore[:, i % 2, :]
                        else:
                            out, src = negmax[:, par, :, i], pscore[:, i % 2, :].rearrange("p (q k) -> p q k", q=QT)
                        nc.vector.tensor_reduce(out, src, AX.X, ALU.max, negate=True).then_inc(max_done, 1)
                        if i == 1 and cross and runs(b, t, 5):
                            invert(1, g - 5)
                            normalise(b, t)
                        if cross and i >= 2:
                            key_low(b, t, i - 2)
                elif cross:
                    if runs(b, t, 5):
                        invert(1, g - 5)
                        normalise(b, t)
                    for h in range(2):
                        key_low(b, t, h)
                if not cross:
                    for h in range(2):
                        key_low(b, t, h)
                if t == PAIRS - 1 and cross and not is_last(b):
                    lo_ctx(b + 1)
                if runs(b, t, 0):
                    for h in range(2):
                        dve.wait_ge(q_hi, 2 * g + h + 1)
                        last = nc.vector.tensor_tensor(q2[own[h], buf, h, :], pa[own[h], 0:SQ],
                                                       q1[own[h], buf, h, :].bitcast(FP32), ALU.subtract)
                    last.then_inc(q_split, 1)
                if runs(b, t, 0) and t == PAIRS - 1 and not is_last(b) and not cross:
                    ln.dve_lo(dve, b + 1)
                if has_output(b, t):
                    m = b if t == HALF + 4 else (B - 1 if t >= PAIRS else b - 1)
                    dve.wait_ge(y_ready, outputs(b, t))
                    dve.wait_ge(ln.biased, m + 1)
                    nc.vector.tensor_tensor(xs[:, m], xs[:, m], py[:, 0:QT * C].rearrange("p (q c) -> p q c", q=QT),
                                            ALU.add).then_inc(y_taken, 1)
                if runs(b, t, 0) and not is_last(b):
                    if t == 2:
                        ln.dve_stats(dve, b + 1)
                    if t == 4:
                        ln.dve_xhat(dve, b + 1)
                    if t == 6:
                        ln.dve_n32(dve, b + 1)

            nc.vector.memset(ones[:], 1.0).then_inc(ones_set, 1)
            low = lambda which: weights.low(dve, nc.vector.tensor_tensor, pieces, which)
            ln.dve_stats(dve, 0)
            low(DVE_PIECES[:1])
            dve.wait_ge(small_in, 32)
            ln.dve_xhat(dve, 0)
            low(DVE_PIECES[1:2])
            ln.dve_n32(dve, 0)
            low(DVE_PIECES[2:])
            ln.dve_lo(dve, 0)
            if cross:
                lo_ctx(0)
            over_batches(dve, lambda b: [step(b, t) for t in range(PAIRS)])
            tail(step)

        @block.gpsimd
        def _(pool):
            def key_sums(b, t, h):
                g3, par = PAIRS * b + t - 3, (t - 3) % 2
                if h == 0:
                    wait(pool, pv_done, g3 - 1)
                pool.wait_ge(exp_done, NB * g3 + (h + 1) * KB)
                src = probs[:, par, h]
                if cross:
                    wait(pool, sum_ready, 2 * g3 + h)
                    nc.gpsimd.tensor_tensor(half_sum[:, h], src[:, 0:2], src[:, 2:4], ALU.add).then_inc(half_done, 1)
                    wait(pool, half_done, 2 * g3 + h + 1)
                    src = half_sum[:, h]
                nc.gpsimd.tensor_tensor(key_sum[:, par, h], src[:, 0], src[:, 1], ALU.add).then_inc(sum_ready, 1)

            def step(b, t):
                for h in range(2):
                    if runs(b, t, 3):
                        key_sums(b, t, h)
                if runs(b, t, 0) and t == 3 and not is_last(b):
                    ln.pool_rstd(pool, b + 1)

            ln.pool_setup(pool)
            ln.pool_rstd(pool, 0)
            pool.wait_ge(ln.rstd_ready, 1)
            weights.low(pool, nc.gpsimd.tensor_tensor, pieces, POOL_PIECES)
            pool.wait_ge(weights.done, len(pieces))
            for zeroed, place in ((k2_zeroed, k2), (q2_zeroed, q2)):
                for h in range(2):
                    nc.gpsimd.memset(place[other[h], :, h, :].bitcast(FP32), 0.0).then_inc(zeroed, 1)
                    pool.wait_ge(zeroed, h + 1)
            over_batches(pool, lambda b: [step(b, t) for t in range(PAIRS)])
            tail(step)


GROUP = 4
GROUPS = HEADS // GROUP
ROWS = P // GROUP


def narrow_attention_layer(nc, tag, xs, ident, dram, x_t, ctx_t, weights, load_first, first_in, load_next):
    KT = SK // P
    NB = GROUP * KT // 2
    NS = GROUP * QT
    STEPS = 2 * GROUPS
    TURNS = B // 2
    SCALE = float(D0) ** -0.5
    total = GROUPS * B
    WIDE = GROUPS * P

    with ExitStack() as ctx:
        sb = lambda name, shape, dt: ctx.enter_context(nc.sbuf_tensor(f"{tag}_{name}", shape, dt))
        ps = lambda name, shape: ctx.enter_context(nc.psum_tensor(f"{tag}_{name}", shape, FP32))
        sem = lambda name: ctx.enter_context(nc.semaphore(f"{tag}_{name}"))

        wq = sb("wq", [P, 3, WIDE], FP32R)
        wk = sb("wk", [P, 4, WIDE], FP32R)
        wk_ip = sb("wk_ip", [P, 4, WIDE], FP32R)
        wv = sb("wv", [P, 4, 2 * C], FP32R)
        wo = sb("wo", [P, GROUPS, C], FP32)
        bo_rows = sb("bo_rows", [P, QT, C], FP32)
        marks = sb("marks", [P, 12], FP32)
        q_lo, q_sign, k_lo, k_sign = (marks[:, i:i + 1] for i in range(4))
        head_mask = [marks[:, 4 + j:5 + j] for j in range(GROUP)]
        is_text, is_ip = marks[:, 8:9], marks[:, 9:10]
        text_row, ip_row = marks[:, 10:11], marks[:, 11:12]
        pick = sb("pick", [P, P], FP32)
        x32 = sb("x32", [P, 2, SQ], FP32)
        nt = sb("nt", [P, 3, SQ], FP32R)
        ct32 = sb("ct32", [P, 2, SK], FP32)
        ct = sb("ct", [P, 4, SK], FP32R)
        q_signed = sb("q_signed", [P, SQ], FP32R)
        k_signed = sb("k_signed", [P, SK], FP32R)
        q4 = sb("q4", [P, SQ], FP32)
        qm = sb("qm", [P, GROUPS, GROUP, SQ], FP32R)
        k4 = sb("k4", [P, GROUPS, SK], FP32R)
        v = sb("v", [P, 2, KT, HEADS, ROWS], FP32)
        negmax = sb("negmax", [P, 2, QT, GROUP, ROWS], FP32)
        probs = sb("probs", [P, 2, GROUP, KT, SQ], FP32)
        sums = sb("sums", [P, 2, SQ], FP32)
        recip = sb("recip", [P, SQ], FP32)
        ot = sb("ot", [P, GROUPS, SQ], FP32)
        pa, pb, pv, pd = ps("pa", [P, 512]), ps("pb", [P, 512]), ps("pv", [P, 512]), ps("pd", [P, 512])
        pscore = ps("pscore", [P, 2, 512])
        pst = ps("pst", [P, 2, 512])

        small_in = sem("small_in")
        v_cleared, v_marked, consts_set = sem("v_cleared"), sem("v_marked"), sem("consts_set")
        x_in, ctx_in, in_hi, in_ready = sem("x_in"), sem("ctx_in"), sem("in_hi"), sem("in_ready")
        q_ready, k_ready, a_rounded, b_rounded = sem("q_ready"), sem("k_ready"), sem("a_rounded"), sem("b_rounded")
        q4_done, qm_ready, k4_ready = sem("q4_done"), sem("qm_ready"), sem("k4_ready")
        v_ready, v_copied = sem("v_ready"), sem("v_copied")
        score_ready, max_done = sem("score_ready"), sem("max_done")
        max_turned, max_placed = sem("max_turned"), sem("max_placed")
        st_ready, exp_done = sem("st_ready"), sem("exp_done")
        pv_done, sums_copied, den_ready = sem("pv_done"), sem("sums_copied"), sem("den_ready")
        recip_done, ot_ready = sem("recip_done"), sem("ot_ready")
        biased, y_ready, y_taken = sem("biased"), sem("y_ready"), sem("y_taken")

        pieces = n_weight_pieces(dram["wq"], dram["wq_ext"], wq)
        for w, src in ((wk, dram["wk"]), (wk_ip, dram["wk_ip"]), (wv, dram["wv"])):
            for half in range(2):
                pieces.append((src[half], P, w[:, half, :], w[:, 2 + half, :], (0, P)))

        def runs(a, t, lag):
            return not isinstance(a, int) or 0 <= STEPS * a + t - lag < total

        def turns(eng, step, lags):
            for t in range(STEPS):
                step(0, t)
            with eng.Fori(1, TURNS - 1) as a:
                for t in range(STEPS):
                    step(a, t)
            for t in range(STEPS + lags):
                step(TURNS - 1, t)

        def new_batch(a, t):
            if t % GROUPS != GROUPS - 1 or (isinstance(a, int) and STEPS * a + t >= total - 1):
                return None
            return 2 * a + t // GROUPS + 1

        block = ctx.enter_context(nc.Block())

        @block.sync
        def _(sp):
            sp.dma_start(x32[:], x_t[0]).then_inc(x_in, 16)
            sp.dma_start(ct32[:], ctx_t[0]).then_inc(ctx_in, 16)
            weights.load(sp, weight_sources(dram, ["wq"], ["wk", "wk_ip", "wv"]))
            load_first(sp)
            for place, name in ((marks, "marks"), (pick, "pick"), (wo, "wo"), (bo_rows, "bo_rows")):
                sp.dma_start(place[:], dram[name]).then_inc(small_in, 16)
            sp.wait_ge(weights.done, len(pieces))
            load_next(sp)
            with sp.Fori(1, B) as b:
                sp.wait_ge(in_ready, b)
                sp.dma_start(x32[:], x_t[b]).then_inc(x_in, 16)
                sp.dma_start(ct32[:], ctx_t[b]).then_inc(ctx_in, 16)

        @block.tensor
        def _(pe):
            mm = nc.tensor.matmul

            def score(a, t, i):
                g1, buf, j, qt = STEPS * a + t - 1, (t - 1) % GROUPS, i // QT, i % QT
                if i == 0:
                    wait(pe, k4_ready, g1 + 1)
                if qt == 0:
                    wait(pe, qm_ready, GROUP * g1 + j + 1)
                wait(pe, max_done, NS * g1 + i - 1)
                mm(pscore[:, i % 2, :], qm[:, buf, j, qt * P:(qt + 1) * P], k4[:, buf, :],
                   start=True, stop=True).then_inc(score_ready, 1)

            def turned_scores(a, t, n):
                g2, buf, j, kb = STEPS * a + t - 2, (t - 2) % GROUPS, n // (KT // 2), n % (KT // 2)
                if kb == 0:
                    wait(pe, max_placed, GROUP * g2 + j + 1)
                wait(pe, exp_done, NB * g2 + n - 1)
                for i in range(2):
                    kt = 2 * kb + i
                    last = mm(pst[:, n % 2, i * SQ:(i + 1) * SQ], k4[:, buf, kt * P:(kt + 1) * P],
                              qm[:, buf, j, :], start=True, stop=True)
                last.then_inc(st_ready, 1)

            def project(out, w, rows_cols, acts, terms, which):
                for i in which:
                    ws, xs_, rows = terms[i]
                    last = mm(out, w[0:rows, ws, rows_cols], acts(xs_, rows), start=i == 0, stop=i == len(terms) - 1)
                return last

            def projections(a, t, n):
                g, u = STEPS * a + t, t % GROUPS
                b, cols = 2 * a + t // GROUPS, slice(u * P, (u + 1) * P)
                if n == 0:
                    if u == 0:
                        pe.wait_ge(in_ready, b + 1)
                    if u == 3:
                        pe.wait_ge(v_copied, KT * (b + 1))
                    else:
                        wait(pe, q4_done, g)
                    project(pa[:, 0:SQ], wq, cols, lambda s, r: nt[0:r, s, :], N_TERMS, range(4))
                elif n == 1:
                    project(pa[:, SQ:2 * SQ], wk, cols, lambda s, r: ct[0:r, s, 0:SQ], CTX_TERMS,
                            range(6)).then_inc(q_ready, 1)
                else:
                    if n == 2:
                        if u != 3:
                            wait(pe, k4_ready, g)
                        wait(pe, max_placed, GROUP * (g - 1))
                    last = project(pb[:], wk_ip, cols, lambda s, r: ct[0:r, s, :], CTX_TERMS,
                                   range(3 * n - 6, 3 * n - 3))
                    if n == 3:
                        last.then_inc(k_ready, 1)

            def weighted_sums(a, t, kt):
                g3, par, u3 = STEPS * a + t - 3, (t - 3) % 2, (t - 3) % GROUPS
                vb = (t - 3) // GROUPS % 2
                if kt == 0:
                    if u3 == 0:
                        wait(pe, v_copied, KT * ((2 * a + t // GROUPS if t < STEPS else B - 1) + 1))
                    wait(pe, sums_copied, g3)
                    wait(pe, exp_done, NB * (g3 + 1))
                for j in range(GROUP):
                    last = mm(pv[j * ROWS:(j + 1) * ROWS, 0:SQ], v[:, vb, kt, GROUP * u3 + j, :],
                              probs[:, par, j, kt, :], start=kt == 0, stop=kt == KT - 1)
                if kt == KT - 1:
                    last.then_inc(pv_done, 1)

            def step(a, t):
                g = STEPS * a + t
                u = t % GROUPS
                with_output = runs(a, t, 5) and (t - 5) % GROUPS == GROUPS - 1
                for n in range(NB):
                    if runs(a, t, 1):
                        score(a, t, n)
                    if runs(a, t, 0) and n < 4:
                        projections(a, t, n)
                    if runs(a, t, 2):
                        turned_scores(a, t, n)
                    if runs(a, t, 3) and n >= 4:
                        weighted_sums(a, t, n - 4)
                    if n == 3 and with_output:
                        wait(pe, ot_ready, g - 4)
                        for qt in range(QT):
                            for u5 in range(GROUPS):
                                last = mm(pd[:, qt * C:(qt + 1) * C], ot[:, u5, qt * P:(qt + 1) * P], wo[:, u5, :],
                                          start=u5 == 0, stop=u5 == GROUPS - 1)
                        last.then_inc(y_ready, 1)
                    if n == (5 if u == GROUPS - 1 else 4) and runs(a, t, 4):
                        g4, par = g - 4, t % 2
                        if (t - 4) % GROUPS == 0:
                            wait(pe, y_taken, 2 * a + (t - 4) // GROUPS)
                        else:
                            wait(pe, ot_ready, g4)
                        wait(pe, sums_copied, g4 + 1)
                        mm(pd[:, 0:SQ], pick[:], sums[:, par, :], start=True, stop=True).then_inc(den_ready, 1)
                if runs(a, t, 1):
                    if runs(a, t, 0):
                        wait(pe, k4_ready, g + 1)
                    wait(pe, max_done, NS * g)
                    for qt in range(QT):
                        last = nc.tensor.transpose(pb[:, qt * P:(qt + 1) * P],
                                                   negmax[:, (t - 1) % 2, qt].rearrange("p j r -> p (j r)"), ident)
                    last.then_inc(max_turned, 1)
                if runs(a, t, 0) and u == 2:
                    b = 2 * a + t // GROUPS
                    pe.wait_ge(q4_done, g + 1)
                    for kt in range(KT):
                        if kt == 1:
                            pe.wait_ge(max_placed, GROUP * g)
                        if kt >= 2:
                            pe.wait_ge(v_copied, KT * b + kt - 1)
                        for i, (ws, xs_, rows) in enumerate(CTX_TERMS):
                            last = mm((pa, pb)[kt % 2][:, 0:2 * C], ct[0:rows, xs_, kt * P:(kt + 1) * P],
                                      wv[0:rows, ws, :], start=i == 0, stop=i == len(CTX_TERMS) - 1)
                        last.then_inc(v_ready, 1)

            pe.wait_ge(consts_set, 1)
            pe.wait_ge(small_in, 64)
            pe.wait_ge(weights.done, len(pieces))
            pe.wait_ge(*first_in)
            turns(pe, step, 6)

        @block.scalar
        def _(act):
            def hi_inputs(m, part):
                if part == 0:
                    act.wait_ge(x_in, 16 * (m + 1))
                    nc.scalar.activation(nt[:, 0], x32[:, 0], ACT.Copy)
                    nc.scalar.activation(nt[0:EXT, 2], x32[0:EXT, 1], ACT.Copy).then_inc(in_hi, 1)
                    return
                act.wait_ge(ctx_in, 16 * (m + 1))
                nc.scalar.activation(ct[:, part - 1], ct32[:, part - 1], ACT.Copy).then_inc(in_hi, 1)

            def exp(a, t, n):
                g2, par, j, kb = STEPS * a + t - 2, t % 2, n // (KT // 2), n % (KT // 2)
                if n == 0:
                    wait(act, pv_done, g2 - 1)
                act.wait_ge(st_ready, NB * g2 + n + 1)
                nc.scalar.activation(probs[:, par, j, 2 * kb:2 * kb + 2, :],
                                     pst[:, n % 2, :].rearrange("p (k q) -> p k q", k=2),
                                     ACT.Exp, scale=SCALE).then_inc(exp_done, 1)

            def masked_q(a, t, heads):
                act.wait_ge(q4_done, STEPS * a + t + 1)
                for j in heads:
                    nc.scalar.activation(qm[:, t % GROUPS, j, :], q4[:], ACT.Copy,
                                         scale=head_mask[j]).then_inc(qm_ready, 1)

            def step(a, t):
                g = STEPS * a + t
                u = t % GROUPS
                for n in range(NB):
                    if runs(a, t, 2):
                        exp(a, t, n)
                    if runs(a, t, 0):
                        if n == 1:
                            act.wait_ge(q_ready, g + 1)
                            nc.scalar.activation(q_signed[:], pa[:, 0:SQ], ACT.Copy, scale=q_sign)
                            nc.scalar.activation(k_signed[:, 0:TEXT], pa[:, SQ:SQ + TEXT], ACT.Identity,
                                                 scale=k_sign, bias=text_row).then_inc(a_rounded, 1)
                        if n == 3:
                            act.wait_ge(k_ready, g + 1)
                            nc.scalar.activation(k_signed[:, TEXT:SK], pb[:, TEXT:SK], ACT.Identity,
                                                 scale=k_sign, bias=ip_row).then_inc(b_rounded, 1)
                            masked_q(a, t, (0, 1))
                        if n == 4:
                            masked_q(a, t, (2, 3))
                        if n >= 5 and new_batch(a, t) is not None:
                            hi_inputs(new_batch(a, t), n - 5)
                if runs(a, t, 1):
                    act.wait_ge(max_turned, g)
                    for j in range(GROUP):
                        rows = slice(j * ROWS, j * ROWS + 2)
                        nc.scalar.activation(qm[rows, (t - 1) % GROUPS, j, :], pb[rows, 0:SQ],
                                             ACT.Copy).then_inc(max_placed, 1)
                if runs(a, t, 3):
                    g3, par = g - 3, (t - 3) % 2
                    act.wait_ge(pv_done, g3 + 1)
                    wait(act, ot_ready, g3 - 1)
                    nc.scalar.activation(sums[:, par, :], pv[:, 0:SQ], ACT.Copy).then_inc(sums_copied, 1)
                if runs(a, t, 0) and u == 2:
                    b, vb = 2 * a + t // GROUPS, t // GROUPS
                    for kt in range(KT):
                        act.wait_ge(v_ready, KT * b + kt + 1)
                        src = (pa, pb)[kt % 2]
                        heads = lambda i: src[:, i * C:(i + 1) * C].rearrange("p (h d) -> p h d", d=D0)
                        ip = v[:, vb, kt, :, D0:2 * D0]
                        if kt == 0:
                            nc.scalar.activation(v[:, vb, 0, :, 0:D0], heads(0), ACT.Copy, scale=is_text)
                            last = nc.scalar.activation(ip, heads(1), ACT.Copy, scale=is_ip)
                        else:
                            last = nc.scalar.activation(ip, heads(1), ACT.Copy)
                        last.then_inc(v_copied, 1)

            for part in range(3):
                hi_inputs(0, part)
            weights.high(act, pieces)
            act.wait_ge(small_in, 64)
            act.wait_ge(v_marked, 1)
            turns(act, step, 6)

        @block.vector
        def _(dve):
            def lo_inputs(m, part):
                dve.wait_ge(in_hi, 3 * m + part + 1)
                minus = lambda out, x, hi: nc.vector.tensor_tensor(out, x, hi.bitcast(FP32), ALU.subtract)
                if part == 0:
                    minus(nt[:, 1], x32[:, 0], nt[:, 0])
                    minus(nt[2 * REST:EXT, 2], x32[2 * REST:EXT, 1], nt[2 * REST:EXT, 2])
                else:
                    last = minus(ct[:, 1 + part], ct32[:, part - 1], ct[:, part - 1])
                    if part == 2:
                        last.then_inc(in_ready, 1)

            def maximum(a, t, i):
                g1, par, j, qt = STEPS * a + t - 1, (t - 1) % 2, i // QT, i % QT
                dve.wait_ge(score_ready, NS * g1 + i + 1)
                for s, keys in enumerate((slice(0, TEXT), slice(TEXT, SK))):
                    last = nc.vector.tensor_reduce(negmax[:, par, qt, j, s:s + 1], pscore[:, i % 2, keys],
                                                   AX.X, ALU.max, negate=True)
                last.then_inc(max_done, 1)

            def invert(a, t, half):
                g4, part = STEPS * a + t - 4, slice(half * SQ // 2, (half + 1) * SQ // 2)
                if half == 0:
                    wait(dve, ot_ready, g4)
                    dve.wait_ge(den_ready, g4 + 1)
                nc.vector.reciprocal(recip[:, part], pd[:, part]).then_inc(recip_done, 1)

            def step(a, t):
                g = STEPS * a + t
                fuse = nc.vector.scalar_tensor_tensor
                buf = t % GROUPS
                busy = t % GROUPS == GROUPS - 1
                for i in range(NS):
                    if runs(a, t, 1):
                        maximum(a, t, i)
                    if i == 2 and runs(a, t, 0):
                        dve.wait_ge(a_rounded, g + 1)
                        fuse(out=q4[:], in0=pa[:, 0:SQ], scalar=q_lo, in1=q_signed[:].bitcast(FP32),
                             op0=ALU.mult, op1=ALU.add)
                        fuse(out=k4[:, buf, 0:TEXT], in0=pa[:, SQ:SQ + TEXT], scalar=k_lo,
                             in1=k_signed[:, 0:TEXT].bitcast(FP32), op0=ALU.mult, op1=ALU.add).then_inc(q4_done, 1)
                    if i == 3 and runs(a, t, 5) and (t - 5) % GROUPS == GROUPS - 1:
                        m = 2 * a + (t - 5) // GROUPS
                        nc.vector.tensor_tensor(xs[:, m], xs[:, m], bo_rows[:], ALU.add).then_inc(biased, 1)
                        dve.wait_ge(biased, m + 1)
                        dve.wait_ge(y_ready, m + 1)
                        nc.vector.tensor_tensor(xs[:, m], xs[:, m],
                                                pd[:, 0:QT * C].rearrange("p (q c) -> p q c", q=QT),
                                                ALU.add).then_inc(y_taken, 1)
                    if i == 4 and runs(a, t, 0):
                        dve.wait_ge(b_rounded, g + 1)
                        fuse(out=k4[:, buf, TEXT:SK], in0=pb[:, TEXT:SK], scalar=k_lo,
                             in1=k_signed[:, TEXT:SK].bitcast(FP32), op0=ALU.mult, op1=ALU.add).then_inc(k4_ready, 1)
                    if i >= 5 and new_batch(a, t) is not None:
                        lo_inputs(new_batch(a, t), i - 5)
                    if i == (NS - 1 if busy else 5) and runs(a, t, 4):
                        invert(a, t, 0)
                    if i == (NS - 1 if busy else 7) and runs(a, t, 4):
                        invert(a, t, 1)
                    if i == (NS - 1 if busy else 7) and runs(a, t, 4):
                        dve.wait_ge(recip_done, 2 * (g - 3))
                        nc.vector.tensor_tensor(ot[:, (t - 4) % GROUPS, :], sums[:, t % 2, :], recip[:],
                                                ALU.mult).then_inc(ot_ready, 1)

            for part in range(3):
                lo_inputs(0, part)
            weights.low(dve, nc.vector.tensor_tensor, pieces, range(len(pieces)))
            dve.wait_ge(small_in, 64)
            dve.wait_ge(v_cleared, 2)
            for vb in range(2):
                nc.vector.memset(v[:, vb, 1:KT, :, 3 * D0:4 * D0], 1.0)
                for s in range(2):
                    cols = slice((2 + s) * D0, (3 + s) * D0)
                    last = nc.vector.tensor_scalar(v[:, vb, 0, :, cols], v[:, vb, 0, :, cols],
                                                   marks[:, 8 + s:9 + s], None, ALU.add)
            last.then_inc(v_marked, 1)
            dve.wait_ge(*first_in)
            dve.wait_ge(consts_set, 1)
            turns(dve, step, 6)

        @block.gpsimd
        def _(pool):
            nc.gpsimd.memset(negmax[:], 0.0).then_inc(consts_set, 1)
            for vb in range(2):
                nc.gpsimd.memset(v[:, vb], 0.0).then_inc(v_cleared, 1)


def feed_forward_layer(nc, tag, xs, ident, dram, out, raw):
    FT = FF // P

    with ExitStack() as ctx:
        sb = lambda name, shape, dt: ctx.enter_context(nc.sbuf_tensor(f"{tag}_{name}", shape, dt))
        ps = lambda name, shape: ctx.enter_context(nc.psum_tensor(f"{tag}_{name}", shape, FP32))
        sem = lambda name: ctx.enter_context(nc.semaphore(f"{tag}_{name}"))

        w1 = sb("w1", [P, 3, 2 * FF], FP32R)
        w2 = sb("w2", [P, FT, C], FP32)
        b1 = sb("b1", [P, 2 * FT], FP32)
        b2_rows = sb("b2_rows", [P, QT, C], FP32)
        gains = sb("gains", [P, 4], FP32)
        nt = sb("nt", [P, 3, SQ], FP32R)
        gate = sb("gate", [P, FT, SQ], FP32)
        hidden = sb("hidden", [P, FT, SQ], FP32)
        ph = ps("ph", [P, FT, 512])
        pt, py = ps("pt", [P, 512]), ps("py", [P, 512])

        small_in = sem("small_in")
        h_ready, gelu_done, hidden_ready = sem("h_ready"), sem("gelu_done"), sem("hidden_ready")
        y_ready, y_taken, stored = sem("y_ready"), sem("y_taken"), sem("stored")

        ln = LayerNorm(nc, ctx, f"{tag}_ln", xs, ident, nt, gains, b2_rows[:], pt)
        weights = Weights(nc, ctx, tag, raw, 2 * FF, 2, True)
        pieces = n_weight_pieces(dram["w1"], dram["w1_ext"], w1)
        block = ctx.enter_context(nc.Block())

        @block.sync
        def _(sp):
            weights.load(sp, weight_sources(dram, ["w1"], []))
            for place, name in ((gains, "gains"), (b2_rows, "b2_rows"), (b1, "b1"), (w2, "w2")):
                sp.dma_start(place[:], dram[name]).then_inc(small_in, 16)
            with sp.Fori(0, B) as b:
                sp.wait_ge(y_taken, b + 1)
                sp.dma_start(out[b], xs[:, b]).then_inc(stored, 16)
            sp.wait_ge(stored, 16 * B)

        @block.tensor
        def _(pe):
            mm = nc.tensor.matmul

            def batch(b):
                pe.wait_ge(ln.n_ready, b + 1)
                for i in range(FT):
                    wait(pe, hidden_ready, FT * (b - 1) + i + 1)
                    for s in range(2):
                        cols = slice((s * FT + i) * P, (s * FT + i + 1) * P)
                        for k, (ws, xs_, rows) in enumerate(N_TERMS):
                            last = mm(ph[:, i, s * SQ:(s + 1) * SQ], w1[0:rows, ws, cols], nt[0:rows, xs_, :],
                                      start=k == 0, stop=k == len(N_TERMS) - 1)
                    last.then_inc(h_ready, 1)
                if not is_last(b):
                    ln.pe_transpose(pe, b + 1)
                wait(pe, y_taken, b)
                for qt in range(QT):
                    for i in range(FT):
                        pe.wait_ge(hidden_ready, FT * b + i + 1)
                        last = mm(py[:, qt * C:(qt + 1) * C], hidden[:, i, qt * P:(qt + 1) * P], w2[:, i, :],
                                  start=i == 0, stop=i == FT - 1)
                last.then_inc(y_ready, 1)

            pe.wait_ge(small_in, 64)
            ln.pe_transpose(pe, 0)
            pe.wait_ge(weights.done, len(pieces))
            over_batches(pe, batch)

        @block.scalar
        def _(act):
            def batch(b):
                for i in range(FT):
                    act.wait_ge(h_ready, FT * b + i + 1)
                    nc.scalar.activation(gate[:, i, :], ph[:, i, SQ:2 * SQ], ACT.Gelu,
                                         bias=b1[:, FT + i:FT + i + 1]).then_inc(gelu_done, 1)
                if not is_last(b):
                    ln.act_hi(act, b + 1)

            weights.high(act, pieces)
            act.wait_ge(small_in, 64)
            ln.act_hi(act, 0)
            over_batches(act, batch)

        @block.vector
        def _(dve):
            def batch(b):
                if not is_last(b):
                    ln.dve_stats(dve, b + 1)
                    ln.dve_xhat(dve, b + 1)
                for i in range(FT):
                    dve.wait_ge(gelu_done, FT * b + i + 1)
                    nc.vector.scalar_tensor_tensor(out=hidden[:, i, :], in0=ph[:, i, 0:SQ], scalar=b1[:, i:i + 1],
                                                   in1=gate[:, i, :], op0=ALU.add,
                                                   op1=ALU.mult).then_inc(hidden_ready, 1)
                if not is_last(b):
                    ln.dve_n32(dve, b + 1)
                    ln.dve_lo(dve, b + 1)
                dve.wait_ge(y_ready, b + 1)
                dve.wait_ge(ln.biased, b + 1)
                nc.vector.tensor_tensor(xs[:, b], xs[:, b], py[:, 0:QT * C].rearrange("p (q c) -> p q c", q=QT),
                                        ALU.add).then_inc(y_taken, 1)

            dve.wait_ge(small_in, 64)
            ln.dve_stats(dve, 0)
            ln.dve_xhat(dve, 0)
            ln.dve_n32(dve, 0)
            weights.low(dve, nc.vector.tensor_tensor, pieces, range(len(pieces)))
            ln.dve_lo(dve, 0)
            over_batches(dve, batch)

        @block.gpsimd
        def _(pool):
            ln.pool_setup(pool)
            ln.pool_rstd(pool, 0)
            with pool.Fori(1, B) as b:
                ln.pool_rstd(pool, b)


def build(nc, t, out):
    with ExitStack() as ctx:
        xs = ctx.enter_context(nc.sbuf_tensor("xs", [P, B, QT, C], FP32))
        ident = ctx.enter_context(nc.sbuf_tensor("identity", [P, P], FP32))
        raw = ctx.enter_context(nc.sbuf_tensor("raw_weights", [P, 6 * INNER], FP32))
        weights = {"l0": Weights(nc, ctx, "l0", raw, GROUPS * P, 8, True),
                   "a1": Weights(nc, ctx, "a1", raw, INNER, 6, False),
                   "a2": Weights(nc, ctx, "a2", raw, INNER, 6, False)}
        inputs_in = ctx.enter_context(nc.semaphore("inputs_in"))

        def load_first(sp):
            sp.dma_start(ident[:], t["ident"]).then_inc(inputs_in, 16)
            with sp.Fori(0, B) as b:
                sp.dma_start(xs[:, b], t["x"][b]).then_inc(inputs_in, 16)

        load_a1 = lambda sp: weights["a1"].load(sp, weight_sources(t["a1"], ["wq", "wk", "wv"], []))
        load_a2 = lambda sp: weights["a2"].load(sp, weight_sources(t["a2"], ["wq"], ["wk", "wv"]))
        narrow_attention_layer(nc, "l0", xs, ident[:], t["l0"], t["x_t"], t["ctx_t"], weights["l0"],
                               load_first, (inputs_in, 16 * (B + 1)), load_a1)
        attention_layer(nc, "a1", xs, ident[:], t["a1"], None, raw, weights["a1"], load_a2)
        attention_layer(nc, "a2", xs, ident[:], t["a2"], t["ctx_t"], raw, weights["a2"], None)
        feed_forward_layer(nc, "ff", xs, ident[:], t["ff"], out, raw)


def laid_out(inputs):
    x, ctx = inputs["x"], inputs["ctx_2048"]
    halves = lambda w: w.reshape(2, P, w.shape[-1])
    main = lambda w: w[:P]
    ext = lambda w: np.concatenate([w[P:]] * 3)
    rows = lambda bias: np.broadcast_to(bias, (P, QT, C))
    by_tile = lambda w: w.reshape(-1, P, w.shape[-1]).transpose(1, 0, 2)

    arrays = {"ident": np.eye(P, dtype=np.float32),
              "x": x.reshape(B, QT, P, C).transpose(0, 2, 1, 3),
              "ctx_t": ctx.transpose(0, 2, 1).reshape(B, 2, P, SK).transpose(0, 2, 1, 3)}
    x_t = x.transpose(0, 2, 1)
    both = np.zeros((B, P, 2, SQ), np.float32)
    both[:, :, 0] = x_t[:, :P]
    both[:, :EXT, 1] = np.concatenate([x_t[:, P:]] * 3, axis=1)
    arrays["x_t"] = both

    repeat = lambda w: np.broadcast_to(w.reshape(-1, HEADS, 1, D0), (w.shape[0], HEADS, 4, D0)).reshape(w.shape[0], -1)
    w0 = {k: inputs[f"L0_xattn_{k}"].T for k in ("Wq", "Wk", "Wv", "Wk_ip", "Wv_ip", "Wo")}
    wq = repeat(w0["Wq"])
    marks = np.zeros((P, 12), np.float32)
    r = np.arange(P) % ROWS // D0
    marks[:, 0], marks[:, 1] = r == 3, np.array([0, 1, 1, -1])[r]
    marks[:, 2], marks[:, 3] = r == 2, np.array([0, 1, -1, 1])[r]
    marks[0::ROWS, 10], marks[1::ROWS, 11] = 1, 1
    for j in range(GROUP):
        marks[j * ROWS:(j + 1) * ROWS, 4 + j] = 1
    marks[:TEXT, 8] = 1
    marks[TEXT:, 9] = 1
    pick = np.zeros((P, P), np.float32)
    m = np.arange(P)
    pick[np.where(m % ROWS < 2 * D0, m + 2 * D0, m), m] = 1
    wo = np.zeros((GROUPS, GROUP, 4, D0, C), np.float32)
    wo[:, :, 0] = wo[:, :, 1] = w0["Wo"].reshape(GROUPS, GROUP, D0, C)
    layers = {"l0": {"wq": main(wq), "wq_ext": ext(wq), "wk": halves(repeat(w0["Wk"])),
                     "wk_ip": halves(repeat(w0["Wk_ip"])),
                     "wv": halves(np.concatenate([w0["Wv"], w0["Wv_ip"]], axis=1)),
                     "wo": wo.reshape(GROUPS, P, C).transpose(1, 0, 2), "bo_rows": rows(inputs["L0_xattn_bo"]),
                     "marks": marks, "pick": pick}}

    def gains(n):
        g, b = inputs[f"L1_xattn_{n}_g"], inputs[f"L1_xattn_{n}_b"]
        out = np.zeros((P, 4), np.float32)
        out[:, 0], out[:, 1] = g[:P], b[:P]
        out[:EXT, 2], out[:EXT, 3] = np.concatenate([g[P:]] * 3), np.concatenate([b[P:]] * 3)
        return out

    for a, n in (("a1", "ln1"), ("a2", "ln2")):
        w = {k: inputs[f"L1_xattn_{a}_{k}"] for k in ("wq", "wk", "wv", "wo", "bo")}
        layers[a] = {"wq": main(w["wq"]), "wq_ext": ext(w["wq"]), "wo": by_tile(w["wo"]),
                     "bo_rows": rows(w["bo"]), "gains": gains(n)}
        for k in ("wk", "wv"):
            if a == "a1":
                layers[a] |= {k: main(w[k]), k + "_ext": ext(w[k])}
            else:
                layers[a][k] = halves(w[k])
    w1 = inputs["L1_xattn_ff_w1"]
    layers["ff"] = {"w1": main(w1), "w1_ext": ext(w1), "w2": by_tile(inputs["L1_xattn_ff_w2"]),
                    "b1": inputs["L1_xattn_ff_b1"].reshape(-1, P).T, "b2_rows": rows(inputs["L1_xattn_ff_b2"]),
                    "gains": gains("ln3")}
    for layer, named in layers.items():
        arrays |= {f"{layer}.{name}": a for name, a in named.items()}
    return arrays


def kernel(**inputs):
    from concourse import bacc
    from concourse.bass_utils import run_bass_kernel_spmd

    inputs = {k: np.asarray(v) for k, v in inputs.items()}
    arrays = {f"in_{k.replace('.', '_')}": np.ascontiguousarray(a) for k, a in laid_out(inputs).items()}
    nc = bacc.Bacc("TRN2", target_bir_lowering=False, num_devices=1)
    t = {}
    for key in laid_out(inputs):
        name = f"in_{key.replace('.', '_')}"
        a = arrays[name]
        ap = nc.dram_tensor(name, a.shape, mybir.dt.from_np(a.dtype), kind="ExternalInput").ap()
        if "." in key:
            layer, part = key.split(".")
            t.setdefault(layer, {})[part] = ap
        else:
            t[key] = ap
    out = nc.dram_tensor("out", (B, P, QT, C), FP32, kind="ExternalOutput").ap()
    build(nc, t, out)
    r = run_bass_kernel_spmd(nc, [arrays], core_ids=[0])
    return r.results[0]["out"].transpose(0, 2, 1, 3).reshape(B, SQ, C)
```
